# Optimizing a Trainium2 kernel written in Bass

```python
import numpy as np
import jax
import jax.numpy as jnp

def _softmax(x, axis=-1):
    return jax.nn.softmax(x, axis=axis)

def _gelu(x):
    return jax.nn.gelu(x, approximate=True)

def _silu(x):
    return jax.nn.silu(x)

def _sigmoid(x):
    return jax.nn.sigmoid(x)

def _layernorm(x, axis=-1, eps=1e-05):
    m = jnp.mean(x, axis=axis, keepdims=True)
    v = jnp.var(x, axis=axis, keepdims=True)
    return (x - m) / jnp.sqrt(v + eps)

def _scatter_add(tgt, idx, src, axis=0):
    return tgt.at[idx].add(src)

def _segment_sum(src, seg, n):
    return jax.ops.segment_sum(src, seg, n)
kernel_name = 'mk_macaron_d1_jaxref_r8_5e8370'

def setup_inputs(seed: int=0):
    np.random.seed(seed)
    _w = jnp.asarray

    def _L0_attn_setup():
        import jax, jax.numpy as jnp
        import numpy as np
        B, T, D, H = (4, 256, 128, 16)
        E = D // H
        DH = D // 4
        key = jax.random.key(seed)
        ks = jax.random.split(key, 9)
        s = D ** (-0.5)
        return {'x': jax.random.normal(ks[0], (B, T, D), jnp.float32), 'q_w': jax.random.normal(ks[1], (D, D), jnp.float32) * s, 'k_w': jax.random.normal(ks[2], (D, D), jnp.float32) * s, 'v_w': jax.random.normal(ks[3], (D, D), jnp.float32) * s, 'o_w': jax.random.normal(ks[4], (D, D), jnp.float32) * s, 'cs_w1': jax.random.normal(ks[5], (DH, D), jnp.float32) * s, 'cs_b1': jnp.zeros((DH,), jnp.float32), 'cs_w2': jax.random.normal(ks[6], (H, DH), jnp.float32) * DH ** (-0.5), 'cs_b2': jnp.zeros((H,), jnp.float32), 'decay_params': jax.random.normal(ks[7], (H, E), jnp.float32) + 3.0}
    _L0_attn_in = _L0_attn_setup()

    def _L0_ffn_setup():
        import jax, jax.numpy as jnp
        import numpy as np

        def _binarize(w):
            alpha = jax.lax.stop_gradient(jnp.mean(jnp.abs(w), axis=1, keepdims=True))
            bw = alpha * jnp.sign(w)
            return w + jax.lax.stop_gradient(bw - w)
        key = jax.random.key(seed)
        k1, k2, k3, k4, k5 = jax.random.split(key, 5)
        D, H = (128, 512)
        x = jax.random.normal(k1, (64, 196, D), dtype=jnp.float32)
        w1 = jax.random.normal(k2, (H, D), dtype=jnp.float32) * 0.02
        b1 = jax.random.normal(k3, (H,), dtype=jnp.float32) * 0.02
        w2 = jax.random.normal(k4, (D, H), dtype=jnp.float32) * 0.02
        b2 = jax.random.normal(k5, (D,), dtype=jnp.float32) * 0.02
        return {'x': x, 'w1': w1, 'b1': b1, 'w2': w2, 'b2': b2}
    _L0_ffn_in = _L0_ffn_setup()
    _d = {'L0_attn_x': _L0_attn_in['x'], 'L0_attn_q_w': _L0_attn_in['q_w'], 'L0_attn_k_w': _L0_attn_in['k_w'], 'L0_attn_v_w': _L0_attn_in['v_w'], 'L0_attn_o_w': _L0_attn_in['o_w'], 'L0_attn_cs_w1': _L0_attn_in['cs_w1'], 'L0_attn_cs_b1': _L0_attn_in['cs_b1'], 'L0_attn_cs_w2': _L0_attn_in['cs_w2'], 'L0_attn_cs_b2': _L0_attn_in['cs_b2'], 'L0_attn_decay_params': _L0_attn_in['decay_params'], 'L0_ffn_w1': _L0_ffn_in['w1'], 'L0_ffn_b1': _L0_ffn_in['b1'], 'L0_ffn_w2': _L0_ffn_in['w2'], 'L0_ffn_b2': _L0_ffn_in['b2']}
    _x0 = _d['L0_attn_x']
    _d['L0_attn_x'] = jax.random.normal(jax.random.fold_in(jax.random.key(seed), 1), (32, 256, 128), dtype=_x0.dtype)
    del _x0
    return _d

def reference(L0_attn_x, L0_attn_q_w, L0_attn_k_w, L0_attn_v_w, L0_attn_o_w, L0_attn_cs_w1, L0_attn_cs_b1, L0_attn_cs_w2, L0_attn_cs_b2, L0_attn_decay_params, L0_ffn_w1, L0_ffn_b1, L0_ffn_w2, L0_ffn_b2):

    def _L0_attn_ref(x, q_w, k_w, v_w, o_w, cs_w1, cs_b1, cs_w2, cs_b2, decay_params):
        import jax, jax.numpy as jnp
        import numpy as np
        B, T, D, H = (4, 256, 128, 16)
        E = D // H
        DH = D // 4
        Bx, Tx, Dx = x.shape
        q = (x @ q_w.T).reshape(Bx, Tx, H, E)
        k = (x @ k_w.T).reshape(Bx, Tx, H, E)
        v = (x @ v_w.T).reshape(Bx, Tx, H, E)
        lc = jax.nn.sigmoid(jnp.tanh(x @ cs_w1.T + cs_b1) @ cs_w2.T + cs_b2)
        base = jax.nn.sigmoid(decay_params)[None, None]
        lam = jnp.clip(base * (1.0 + 0.2 * lc[..., None]), 0.0, 0.9995)

        def step(state, inp):
            qt, kt, vt, dt = inp
            state = state * dt[..., None] + kt[..., None] * vt[:, :, None, :]
            out_t = jnp.einsum('bhe,bhef->bhf', qt, state)
            return (state, out_t)
        init = jnp.zeros((Bx, H, E, E), x.dtype)
        xs = (jnp.swapaxes(q, 0, 1), jnp.swapaxes(k, 0, 1), jnp.swapaxes(v, 0, 1), jnp.swapaxes(lam, 0, 1))
        _, ys = jax.lax.scan(step, init, xs)
        y = jnp.swapaxes(ys, 0, 1).reshape(Bx, Tx, Dx)
        return y @ o_w.T

    def _L0_ffn_ref(x, w1, b1, w2, b2):
        import jax, jax.numpy as jnp
        import numpy as np

        def _binarize(w):
            alpha = jax.lax.stop_gradient(jnp.mean(jnp.abs(w), axis=1, keepdims=True))
            bw = alpha * jnp.sign(w)
            return w + jax.lax.stop_gradient(bw - w)
        bw1 = _binarize(w1)
        h = jnp.einsum('bsd,hd->bsh', x, bw1) + b1
        h = jax.nn.gelu(h, approximate=False)
        bw2 = _binarize(w2)
        out = jnp.einsum('bsh,dh->bsd', h, bw2) + b2
        return out
    x = L0_attn_x
    x = x + 0.5 * _L0_ffn_ref(_layernorm(x, axis=-1), L0_ffn_w1, L0_ffn_b1, L0_ffn_w2, L0_ffn_b2)
    x = x + _L0_attn_ref(_layernorm(x, axis=-1), L0_attn_q_w, L0_attn_k_w, L0_attn_v_w, L0_attn_o_w, L0_attn_cs_w1, L0_attn_cs_b1, L0_attn_cs_w2, L0_attn_cs_b2, L0_attn_decay_params)
    x = x + 0.5 * _L0_ffn_ref(_layernorm(x, axis=-1), L0_ffn_w1, L0_ffn_b1, L0_ffn_w2, L0_ffn_b2)
    return x

_drawn_inputs = setup_inputs


def setup_inputs(seed=0):
    import zlib

    import numpy as np

    out = dict(_drawn_inputs(seed))
    spreads = {'L0_attn_cs_b1': (0.0, 0.419), 'L0_attn_cs_b2': (0.0, 0.1)}
    factors = {'L0_ffn_b1': 8.0, 'L0_ffn_b2': 4.233}
    for name, (base, spread) in spreads.items():
        noise = np.random.default_rng([zlib.crc32(name.encode()), seed]).standard_normal(out[name].shape)
        drawn = base * np.exp(spread * noise) if base else spread * noise
        out[name] = jnp.asarray(drawn.astype(out[name].dtype))
    for name, factor in factors.items():
        out[name] = (out[name] * factor).astype(out[name].dtype)
    return out
```

```python
from contextlib import ExitStack

import concourse.bass as bass
from concourse import mybir

F32 = mybir.dt.float32
F32R = mybir.dt.float32r
ALU = mybir.AluOpType
ACT = mybir.ActivationFunctionType
AX_X = mybir.AxisListType.X

P = 128
BANK = 512
EPS = 1e-5
LAM_MAX = 0.9995


def macaron(nc, x, q_w, k_w, v_w, o_w, cs_w1, cs_b1, cs_w2, cs_b2, decay, w1, b1, w2, b2, out):
    SEQS, T, D = x.shape
    HEADS, E = decay.shape
    DH = cs_w1.shape[0]
    HID = w1.shape[0]
    TOKENS = SEQS * T
    BLK = 2 * BANK
    TILES = BLK // P
    NB = TOKENS // BLK
    NJ = HID // P
    assert D == P and HEADS * E == P and BLK % T == 0 and NB % 2 == 0 and NB >= 4 and NJ % 2 == 0 and E % 4 == 0
    LAG = 3
    NP = 4

    WORK_FFN = (0, NB * (NJ + E))
    WORK_ATTN = NB * NJ
    TURN_ATTN = 2 * NB
    TURN_FFN2 = TURN_ATTN + 5 + 7 * (NB - 1) + 2

    def turn_ffn(phase, n, what):
        return (0, TURN_FFN2)[phase] + 2 * n + {"out": 0, "in": 1}[what]

    TURN_LAST = turn_ffn(1, NB - 1, "in")

    def turn_first(what):
        return TURN_ATTN + ["q", "k", "v", "c1", "c2"].index(what)

    def turn_attn(n, what, last=False):
        order = ["in", "out"] if last else ["in", "q", "k", "v", "out", "c1", "c2"]
        return TURN_ATTN + 5 + 7 * n + order.index(what)

    with ExitStack() as ctx:
        def sb(name, shape, dt=F32):
            return ctx.enter_context(nc.sbuf_tensor(name, shape, dt))

        def sem(name):
            return ctx.enter_context(nc.semaphore(name))

        turn = ctx.enter_context(nc.psum_tensor("turn", [P, BLK], F32))
        work = ctx.enter_context(nc.psum_tensor("work", [P, 2, BLK], F32))
        acc = ctx.enter_context(nc.psum_tensor("acc", [P, BLK], F32))

        x_res = sb("x_res", [P, NB * TILES, D])
        xn = sb("xn", [P, 2, TILES, D])
        bn = sb("bn", [P, 2, TILES, 6])
        mean = sb("mean", [P, 2, TILES])
        diff = sb("diff", [P, 2, TILES])
        var_eps = sb("var_eps", [P, 2, TILES])
        rstd = sb("rstd", [P, 2, TILES])
        minus_half = sb("minus_half", [P, TILES])
        xT_hi = sb("xT_hi", [P, 2, BLK], F32R)
        xT_lo = sb("xT_lo", [P, 2, BLK], F32R)
        gelu = sb("gelu", [P, 2, BLK])
        yT = sb("yT", [P, 2, BLK])
        xT = sb("xT", [P, BLK])
        qT = sb("qT", [P, 2, BLK])
        kT = sb("kT", [P, 2, BLK])
        lam = sb("lam", [P, 2, BLK])
        vT_hi = sb("vT_hi", [P, 2, BLK], F32R)
        vT_lo = sb("vT_lo", [P, 2, BLK], F32R)
        c1 = sb("c1", [DH, BLK])
        c2 = sb("c2", [P, BLK])
        state = sb("state", [P, NP, BLK])
        qS = sb("qS", [P, NP, BLK])

        ident = sb("ident", [P, P])
        w1_sb = sb("w1_sb", [P, NJ, D])
        w2_sb = sb("w2_sb", [P, HID])
        neg1 = sb("neg1", [P, NJ * D])
        sign1 = sb("sign1", [P, NJ, D])
        neg2 = sb("neg2", [P, HID])
        sign2 = sb("sign2", [P, HID])
        abs1 = sb("abs1", [P, NJ, D])
        abs2 = sb("abs2", [P, HID])
        alpha1 = sb("alpha1", [P, NJ])
        alpha2_half = sb("alpha2_half", [P, 1])
        b1_sb = sb("b1_sb", [P, NJ])
        b1_rows = sb("b1_rows", [NJ, P])
        b2_sb = sb("b2_sb", [P, 1])
        b2_half = sb("b2_half", [P, 1])
        sign1T = sb("sign1T", [P, NJ * P], F32R)
        sign2T = sb("sign2T", [P, NJ * D])
        proj_sb = sb("proj_sb", [P, 4, D])
        projT = sb("projT", [P, 4, P])
        cs_w1_sb = sb("cs_w1_sb", [DH, D])
        cs_w2_sb = sb("cs_w2_sb", [P, DH])
        cs_w1T = sb("cs_w1T", [P, DH])
        cs_w2T = sb("cs_w2T", [DH, P])
        cs_b1_sb = sb("cs_b1_sb", [DH, 1])
        cs_b2_sb = sb("cs_b2_sb", [P, 1])
        cs_b2_half = sb("cs_b2_half", [P, 1])
        decay_sb = sb("decay_sb", [P, 1])
        decay_tanh = sb("decay_tanh", [P, 1])
        lam_scale = sb("lam_scale", [P, 1])
        lam_base = sb("lam_base", [P, 1])
        pick = sb("pick", [P, E, P])
        pick_r = sb("pick_r", [P, E, P], F32R)
        o_wT = sb("o_wT", [P, E, D])

        x_load = [sem("x_load_0"), sem("x_load_1")]
        w_load = sem("w_load")
        x_store = [sem("x_store_0"), sem("x_store_1")]
        consts = sem("consts")
        prep_dve = sem("prep_dve")
        prep_act = sem("prep_act")
        prep_pe = sem("prep_pe")
        bn_done = sem("bn_done")
        stats_done = sem("stats_done")
        moment_step = sem("moment_step")
        rstd_done = sem("rstd_done")
        xn_done = sem("xn_done")
        turn_filled = sem("turn_filled")
        turn_drained = sem("turn_drained")
        xT_hi_done = sem("xT_hi_done")
        work_filled = sem("work_filled")
        work_drained = sem("work_drained")
        gelu_used = sem("gelu_used")
        yT_done = sem("yT_done")
        v_hi_done = sem("v_hi_done")
        lam_step = sem("lam_step")
        kv_done = sem("kv_done")
        qS_done = sem("qS_done")
        qS_used = sem("qS_used")

        x_dram = x.rearrange("s t d -> (s t) d").rearrange("(n p) d -> p n d", p=P)
        out_dram = out.rearrange("s t d -> (s t) d").rearrange("(n p) d -> p n d", p=P)
        HALVES = [slice(0, BANK), slice(BANK, BLK)]

        def blocks(eng, body):
            body(0, 0, True, False)
            with eng.Fori(0, (NB - 4) // 2) as i:
                body(i * 2 + 1, 1, False, False)
                body(i * 2 + 2, 0, False, False)
            for n in range(NB - 3, NB):
                body(n, n % 2, False, n == NB - 1)

        block = ctx.enter_context(nc.Block())

        @block.sync
        def _(sp):
            for n in range(NB):
                if n >= 2:
                    sp.wait_ge(x_load[n % 2], 16 * (n // 2))
                sp.dma_start(x_res[:, n * TILES:(n + 1) * TILES, :],
                             x_dram[:, n * TILES:(n + 1) * TILES, :]).then_inc(x_load[n % 2], 16)
            for n in range(NB):
                sp.wait_ge(turn_drained, (turn_ffn(1, n + 1, "out") if n < NB - 1 else TURN_LAST) + 1)
                if n >= 2:
                    sp.wait_ge(x_store[n % 2], 16 * (n // 2))
                sp.dma_start(out_dram[:, n * TILES:(n + 1) * TILES, :],
                             x_res[:, n * TILES:(n + 1) * TILES, :]).then_inc(x_store[n % 2], 16)
            sp.wait_ge(x_store[0], 16 * (NB // 2))
            sp.wait_ge(x_store[1], 16 * (NB // 2))

        @block.gpsimd
        def _(pool):
            nc.gpsimd.memset(minus_half[:], -0.5).then_inc(consts, 1)
            nc.gpsimd.memset(ident[:], 0.0).then_inc(consts, 1)
            pool.wait_ge(consts, 2)
            nc.gpsimd.affine_select(out=ident[:], in_=ident[:], compare_op=ALU.not_equal, fill=1.0, base=0,
                                    pattern=[[-1, P]], channel_multiplier=1).then_inc(consts, 1)
            pool.wait_ge(consts, 3)

            def inverse_std(g, par):
                pool.wait_ge(stats_done, g + 1)
                nc.gpsimd.tensor_tensor(rstd[:, par, :], var_eps[:, par, :], minus_half[:],
                                        ALU.pow).then_inc(rstd_done, 1)

            inverse_std(0, 0)
            inverse_std(1, 1)

            def ffn(phase):
                def body(n, par, first, last):
                    if not (phase == 1 and last) and not (phase == 1 and isinstance(n, int) and n + 2 >= NB):
                        inverse_std(2 * phase * NB + n + 2, par)
                blocks(pool, body)

            def attn(n, par, first, last):
                for f in range(E):
                    if f == 4:
                        inverse_std(NB + n + 2, par)
                    s = n * E + f
                    pool.wait_ge(work_drained, WORK_ATTN + s + 1)
                    if f == 0:
                        pool.wait_ge(turn_drained, (turn_first("q") if first else turn_attn(n - 1, "q")) + 1)
                    if not (first and f < NP):
                        pool.wait_ge(qS_used, s - NP + 1)
                    nc.gpsimd.tensor_tensor(qS[:, f % NP, :], qT[:, par, :], state[:, f % NP, :],
                                            ALU.mult).then_inc(qS_done, 1)

            ffn(0)
            blocks(pool, attn)
            ffn(1)

        @block.scalar
        def _(act):
            loads = [
                (w1_sb[:], w1.rearrange("(j p) d -> p j d", p=P)), (w2_sb[:], w2),
                (b1_rows[:], b1.rearrange("(j p) -> j p", p=P)), (b2_sb[:], b2.rearrange("(p a) -> p a", a=1)),
                (proj_sb[:, 0, :], q_w), (proj_sb[:, 1, :], k_w), (proj_sb[:, 2, :], v_w), (proj_sb[:, 3, :], o_w),
                (cs_w1_sb[:], cs_w1), (cs_b1_sb[:], cs_b1.rearrange("(p a) -> p a", a=1)),
                (decay_sb[:], decay.rearrange("h (e a) -> (h e) a", a=1)),
                (cs_w2_sb[:], cs_w2.rearrange("h (a c) -> h a c", a=1).broadcast_to([HEADS, E, DH])),
                (cs_b2_sb[:], cs_b2.rearrange("(h a c) -> h a c", a=1, c=1).broadcast_to([HEADS, E, 1])),
            ]
            for dst, src in loads:
                act.dma_start(dst, src).then_inc(w_load, 16)
            act.wait_ge(w_load, 16 * N_LOADS)
            act.wait_ge(prep_pe, 1)
            nc.scalar.copy(sign2T[:], work[:, 0, 0:NJ * P]).then_inc(prep_act, 1)
            nc.scalar.activation(decay_tanh[:], decay_sb[:], ACT.Tanh, scale=0.5).then_inc(prep_act, 1)
            nc.scalar.mul(cs_b2_half[:], cs_b2_sb[:], 0.5).then_inc(prep_act, 1)
            act.wait_ge(prep_pe, 2)
            nc.scalar.copy(projT[:].rearrange("p a b -> p (a b)"), work[:, 1, 0:4 * P]).then_inc(prep_act, 1)
            nc.scalar.copy(cs_w1T[:], work[:, 1, BANK:BANK + DH]).then_inc(prep_act, 1)
            nc.scalar.copy(cs_w2T[:], work[0:DH, 1, BANK + P:BANK + 2 * P]).then_inc(prep_act, 1)
            nc.scalar.copy(b1_sb[:], work[:, 1, BANK + 2 * P:BANK + 2 * P + NJ]).then_inc(prep_act, 1)
            act.wait_ge(prep_pe, 3)
            nc.scalar.copy(o_wT[:].rearrange("p a b -> p (a b)"), work[:, 0, :]).then_inc(prep_act, 1)
            act.wait_ge(prep_dve, PREP_ALL)

            def split_hi(use, par):
                act.wait_ge(turn_filled, use + 1)
                nc.scalar.copy(xT_hi[:, par, :], turn[:]).then_inc(xT_hi_done, 1)

            def keep_xT(use):
                act.wait_ge(turn_filled, use + 1)
                nc.scalar.copy(xT[:], turn[:]).then_inc(turn_drained, 1)

            def result(par, read, count, scale, bias):
                act.wait_ge(read, count)
                if scale is None:
                    nc.scalar.copy(yT[:, par, :], acc[:]).then_inc(yT_done, 1)
                else:
                    nc.scalar.activation(yT[:, par, :], acc[:], ACT.Identity, bias=bias,
                                         scale=scale).then_inc(yT_done, 1)

            def ffn(phase):
                def body(n, par, first, last):
                    for j in range(NJ):
                        s = WORK_FFN[phase] + n * NJ + j
                        act.wait_ge(work_filled, s + 1)
                        if not (first and j < 2):
                            act.wait_ge(gelu_used, phase * NB * NJ + n * NJ + j - 1)
                        nc.scalar.activation(gelu[:, j % 2, :], work[:, j % 2, :], ACT.Gelu,
                                             bias=b1_sb[:, j:j + 1], scale=alpha1[:, j:j + 1]
                                             ).then_inc(work_drained, 1)
                        if j == 0 and not first:
                            result(1 - par, gelu_used, (phase * NB + n) * NJ, alpha2_half[:, 0:1], b2_half[:, 0:1])
                        if j == 2 and not (phase == 1 and last):
                            use = turn_ffn(phase, n, "in")
                            if last:
                                keep_xT(use)
                            else:
                                split_hi(use, 1 - par)
                blocks(act, body)
                result(1, gelu_used, (phase + 1) * NB * NJ, alpha2_half[:, 0:1], b2_half[:, 0:1])

            def project(what, use, par, n):
                act.wait_ge(turn_filled, use + 1)
                if what == "q":
                    if n is not None and not (isinstance(n, int) and n == 0):
                        act.wait_ge(qS_done, n * E)
                    nc.scalar.copy(qT[:, par, :], turn[:]).then_inc(turn_drained, 1)
                elif what == "k":
                    if n is not None and not (isinstance(n, int) and n == 0):
                        act.wait_ge(kv_done, n * E)
                    nc.scalar.copy(kT[:, par, :], turn[:]).then_inc(turn_drained, 1)
                elif what == "v":
                    nc.scalar.copy(vT_hi[:, par, :], turn[:]).then_inc(v_hi_done, 1)
                elif what == "c1":
                    nc.scalar.activation(c1[:], turn[0:DH, :], ACT.Tanh, bias=cs_b1_sb[:, 0:1]
                                         ).then_inc(turn_drained, 1)
                elif what == "c2":
                    if n is not None:
                        act.wait_ge(lam_step, 3 * n + 3)
                    nc.scalar.activation(c2[:], turn[:], ACT.Tanh, bias=cs_b2_half[:, 0:1], scale=0.5
                                         ).then_inc(turn_drained, 1)

            def attn(n, par, first, last):
                for f in range(E):
                    if f == 0:
                        use = turn_attn(n, "in", last)
                        if last:
                            split_hi(use, 1 - par)
                        else:
                            keep_xT(use)
                    if not last:
                        for at, what in ((1, "q"), (2, "k"), (3, "v"), (5, "c1"), (6, "c2")):
                            if f == at:
                                project(what, turn_attn(n, what), 1 - par, n)
                    if f == 3 and not first:
                        result(1 - par, qS_used, n * E, None, None)

            split_hi(0, 0)
            ffn(0)
            for what in ("q", "k", "v", "c1", "c2"):
                project(what, turn_first(what), 0, None)
            blocks(act, attn)
            result(1, qS_used, NB * E, None, None)
            ffn(1)

        @block.vector
        def _(dve):
            step = [0]

            def prep(ins, wait=True):
                ins.then_inc(prep_dve, 1)
                step[0] += 1
                if wait:
                    dve.wait_ge(prep_dve, step[0])

            dve.wait_ge(w_load, 16 * N_LOADS)
            for w, neg, sign in ((w1_sb[:].rearrange("p a b -> p (a b)"), neg1[:], sign1[:].rearrange("p a b -> p (a b)")),
                                 (w2_sb[:], neg2[:], sign2[:])):
                prep(nc.vector.tensor_scalar(neg, w, 0.0, None, ALU.is_lt))
                prep(nc.vector.scalar_tensor_tensor(sign, w, 0.0, neg, ALU.is_gt, ALU.subtract))
            prep(nc.vector.tensor_tensor(abs1[:], w1_sb[:], sign1[:], ALU.mult), False)
            prep(nc.vector.tensor_tensor(abs2[:], w2_sb[:], sign2[:], ALU.mult))
            prep(nc.vector.tensor_reduce(alpha1[:], abs1[:], AX_X, ALU.add), False)
            prep(nc.vector.tensor_reduce(alpha2_half[:], abs2[:], AX_X, ALU.add))
            prep(nc.vector.tensor_scalar(alpha1[:], alpha1[:], 1.0 / D, None, ALU.mult), False)
            prep(nc.vector.tensor_scalar(alpha2_half[:], alpha2_half[:], 0.5 / HID, None, ALU.mult), False)
            prep(nc.vector.tensor_scalar(b2_half[:], b2_sb[:], 0.5, None, ALU.mult), False)
            dve.wait_ge(consts, 3)
            for f in range(E):
                src = ident[:].rearrange("p (h e) -> p h e", e=E)[:, :, f:f + 1].broadcast_to([P, HEADS, E])
                prep(nc.vector.tensor_copy(pick[:, f, :].rearrange("p (h e) -> p h e", e=E), src), f == E - 1)
            prep(nc.vector.tensor_copy(pick_r[:], pick[:]), False)
            dve.wait_ge(prep_pe, 1)
            prep(nc.vector.tensor_copy(sign1T[:], turn[:, 0:NJ * P]), False)
            dve.wait_ge(prep_act, 2)
            prep(nc.vector.tensor_scalar(decay_tanh[:], decay_tanh[:], 0.5, 0.5, ALU.mult, ALU.add))
            prep(nc.vector.tensor_scalar(lam_scale[:], decay_tanh[:], 0.1, None, ALU.mult), False)
            prep(nc.vector.tensor_scalar(lam_base[:], decay_tanh[:], 1.1, None, ALU.mult), False)
            assert step[0] == PREP_ALL

            def statistics(g, n, par):
                for t in range(TILES):
                    ins = nc.vector.bn_stats(bn[:, par, t, :], x_res[:, tile(n, t), :])
                ins.then_inc(bn_done, 1)
                dve.wait_ge(bn_done, g + 1)
                mean_e, mean_o, m2_e, m2_o = (bn[:, par, :, k] for k in (1, 4, 2, 5))
                nc.vector.tensor_tensor(mean[:, par, :], mean_e, mean_o, ALU.add)
                nc.vector.tensor_tensor(diff[:, par, :], mean_e, mean_o, ALU.subtract)
                nc.vector.scalar_tensor_tensor(var_eps[:, par, :], m2_e, EPS * D, m2_o, ALU.add, ALU.add
                                               ).then_inc(moment_step, 1)
                dve.wait_ge(moment_step, 2 * g + 1)
                nc.vector.tensor_scalar(mean[:, par, :], mean[:, par, :], 0.5, None, ALU.mult)
                nc.vector.scalar_tensor_tensor(diff[:, par, :], diff[:, par, :], 0.25, diff[:, par, :],
                                               ALU.mult, ALU.mult).then_inc(moment_step, 1)
                dve.wait_ge(moment_step, 2 * g + 2)
                nc.vector.scalar_tensor_tensor(var_eps[:, par, :], var_eps[:, par, :], 1.0 / D, diff[:, par, :],
                                               ALU.mult, ALU.add).then_inc(stats_done, 1)

            def normalise(g, n, par):
                dve.wait_ge(rstd_done, g + 1)
                for t in range(TILES):
                    ins = nc.vector.tensor_scalar(xn[:, par, t, :], x_res[:, tile(n, t), :],
                                                  mean[:, par, t:t + 1], rstd[:, par, t:t + 1],
                                                  ALU.subtract, ALU.mult)
                ins.then_inc(xn_done, 1)

            def tile(n, t):
                return bass.ds(n * TILES + t, 1) if not isinstance(n, int) else slice(n * TILES + t, n * TILES + t + 1)

            def tiles(n):
                return bass.ds(n * TILES, TILES) if not isinstance(n, int) else slice(n * TILES, (n + 1) * TILES)

            def add_result(use, n):
                dve.wait_ge(turn_filled, use + 1)
                nc.vector.tensor_tensor(x_res[:, tiles(n), :], x_res[:, tiles(n), :],
                                        turn[:].rearrange("p (t d) -> p t d", d=D), ALU.add
                                        ).then_inc(turn_drained, 1)

            def split_lo(par, count, hi, lo, hi_done):
                dve.wait_ge(hi_done, count)
                nc.vector.tensor_tensor(lo[:, par, :], turn[:], hi[:, par, :].bitcast(F32), ALU.subtract
                                        ).then_inc(turn_drained, 1)

            def next_norm(phase, n, par, part):
                ahead = n + 2
                if isinstance(n, int) and ahead >= NB:
                    ahead -= NB
                    if phase == 2:
                        return
                part(phase * NB + n + 2, ahead, par)

            def ffn(phase):
                def body(n, par, first, last):
                    if not (phase == 0 and first):
                        add_result(turn_ffn(phase, n, "out"), NB - 1 if first else n - 1)
                    next_norm(2 * phase, n, par, statistics)
                    if not last:
                        split_lo(1 - par, phase * NB + n + 2, xT_hi, xT_lo, xT_hi_done)
                    next_norm(2 * phase, n, par, normalise)
                return body

            dve.wait_ge(x_load[0], 16)
            statistics(0, 0, 0)
            dve.wait_ge(x_load[1], 16)
            statistics(1, 1, 1)
            normalise(0, 0, 0)
            normalise(1, 1, 1)
            split_lo(0, 1, xT_hi, xT_lo, xT_hi_done)

            def ffn_first():
                dve.wait_ge(x_load[0], 16 * 2)
                ffn(0)(0, 0, True, False)
                with dve.Fori(0, (NB - 4) // 2) as i:
                    for half in (0, 1):
                        dve.wait_ge(x_load[1 - half], 16 * (i + 2 + half))
                        ffn(0)(i * 2 + 1 + half, 1 - half, False, False)
                for n in range(NB - 3, NB):
                    if n + 2 < NB:
                        dve.wait_ge(x_load[n % 2], 16 * ((n + 2) // 2 + 1))
                    ffn(0)(n, n % 2, False, n == NB - 1)

            def decay_of(use, par, count):
                dve.wait_ge(turn_drained, use + 1)
                nc.vector.tensor_scalar(c2[:], c2[:], lam_scale[:, 0:1], lam_base[:, 0:1], ALU.mult, ALU.add
                                        ).then_inc(lam_step, 1)
                dve.wait_ge(lam_step, count + 1)
                nc.vector.tensor_scalar(lam[:, par, :], c2[:], LAM_MAX, 0.0, ALU.min, ALU.max
                                        ).then_inc(lam_step, 1)
                dve.wait_ge(lam_step, count + 2)
                nc.vector.memset(lam[:, par, :].rearrange("p (s t) -> p s t", t=T)[:, :, 0:1], 0.0
                                 ).then_inc(lam_step, 1)

            def attn(n, par, first, last):
                for f in range(E):
                    s = WORK_ATTN + n * E + f
                    if f == 0:
                        dve.wait_ge(lam_step, n * 3 + 3)
                    dve.wait_ge(work_filled, s + 1)
                    nc.vector.tensor_tensor(work[:, f % 2, :], work[:, f % 2, :], kT[:, par, :], ALU.mult
                                            ).then_inc(kv_done, 1)
                    if not (first and f < NP):
                        dve.wait_ge(qS_done, n * E + f - NP + 1)
                    dve.wait_ge(kv_done, n * E + f + 1)
                    nc.vector.tensor_tensor_scan(state[:, f % NP, :], lam[:, par, :], work[:, f % 2, :], 0.0,
                                                 ALU.mult, ALU.add).then_inc(work_drained, 1)
                    if f == 1:
                        next_norm(1, n, par, statistics)
                    if f == 0 and last:
                        split_lo(1 - par, NB + 1, xT_hi, xT_lo, xT_hi_done)
                    if f == 3 and not last:
                        split_lo(1 - par, n + 2, vT_hi, vT_lo, v_hi_done)
                    if f == 4:
                        add_result(turn_attn(n, "out", last), NB - 1 if first else n - 1)
                    if f == 5:
                        next_norm(1, n, par, normalise)
                    if f == 7 and not last:
                        decay_of(turn_attn(n, "c2"), 1 - par, n * 3 + 3)

            ffn_first()
            split_lo(0, 1, vT_hi, vT_lo, v_hi_done)
            decay_of(turn_first("c2"), 0, 0)
            blocks(dve, attn)
            blocks(dve, ffn(1))
            add_result(TURN_LAST, NB - 1)

        @block.tensor
        def _(pe):
            def turn_tiles(dst, src_of, ins_of=None):
                for t in range(TILES):
                    ins = nc.tensor.transpose(dst[:, t * P:(t + 1) * P], src_of(t), ident[:])
                return ins

            pe.wait_ge(consts, 3)
            pe.wait_ge(prep_dve, SIGNS)
            for j in range(NJ):
                nc.tensor.transpose(turn[:, j * P:(j + 1) * P], sign1[:, j, :], ident[:])
            for j in range(NJ):
                ins = nc.tensor.transpose(work[:, 0, j * P:(j + 1) * P], sign2[:, j * P:(j + 1) * P], ident[:])
            ins.then_inc(prep_pe, 1)
            for j in range(4):
                nc.tensor.transpose(work[:, 1, j * P:(j + 1) * P], proj_sb[:, j, :], ident[:])
            nc.tensor.transpose(work[:, 1, BANK:BANK + DH], cs_w1_sb[:], ident[0:DH, 0:DH])
            nc.tensor.transpose(work[:, 1, BANK + 2 * P:BANK + 2 * P + NJ], b1_rows[:], ident[0:NJ, 0:NJ])
            nc.tensor.transpose(work[0:DH, 1, BANK + P:BANK + 2 * P], cs_w2_sb[:], ident[:]).then_inc(prep_pe, 1)
            pe.wait_ge(prep_act, 4)
            pe.wait_ge(prep_dve, PICKS)
            for f in range(E):
                ins = nc.tensor.matmul(work[:, 0, f * P:(f + 1) * P], pick[:, f, :], projT[:, 3, :],
                                       start=True, stop=True)
            ins.then_inc(prep_pe, 1)
            pe.wait_ge(prep_act, 8)
            pe.wait_ge(prep_dve, PREP_ALL)

            def turn_in(use, g, par):
                pe.wait_ge(xn_done, g + 1)
                if not (isinstance(use, int) and use == 0):
                    pe.wait_ge(turn_drained, use)
                turn_tiles(turn, lambda t: xn[:, par, t, :]).then_inc(turn_filled, 1)

            def turn_out(use, g, par):
                pe.wait_ge(yT_done, g + 1)
                pe.wait_ge(turn_drained, use)
                turn_tiles(turn, lambda t: yT[:, par, t * P:(t + 1) * P]).then_inc(turn_filled, 1)

            def hidden(phase, n, j, par, first):
                s = WORK_FFN[phase] + n * NJ + j
                if not (phase == 0 and first and j < 2):
                    pe.wait_ge(work_drained, s - 1)
                for half in HALVES:
                    w = sign1T[:, j * P:(j + 1) * P]
                    nc.tensor.matmul(work[:, j % 2, half], w, xT_hi[:, par, half], start=True, stop=False)
                    ins = nc.tensor.matmul(work[:, j % 2, half], w, xT_lo[:, par, half], start=False, stop=True)
                ins.then_inc(work_filled, 1)

            def down(phase, n, j, first):
                pe.wait_ge(work_drained, WORK_FFN[phase] + n * NJ + j + 1)
                if j == 0 and not (phase == 0 and first):
                    pe.wait_ge(yT_done, 2 * phase * NB + n)
                for half in HALVES:
                    ins = nc.tensor.matmul(acc[:, half], sign2T[:, j * D:(j + 1) * D], gelu[:, j % 2, half],
                                           start=(j == 0), stop=(j == NJ - 1))
                ins.then_inc(gelu_used, 1)

            def ffn(phase):
                def body(n, par, first, last):
                    for j in range(NJ):
                        if j == 0:
                            use = (turn_ffn(phase, n - 1, "in") if not first
                                   else 0 if phase == 0 else turn_attn(NB - 1, "in", True))
                            pe.wait_ge(turn_drained, use + 1)
                        hidden(phase, n, j, par, first)
                        if j > 0:
                            down(phase, n, j - 1, first)
                        elif not first:
                            down(phase, n - 1, NJ - 1, False)
                        if j == 1 and not (phase == 0 and first):
                            turn_out(turn_ffn(phase, n, "out"), 2 * phase * NB + n - 1, 1 - par)
                        if j == 2 and not (phase == 1 and last):
                            turn_in(turn_ffn(phase, n, "in"), 2 * phase * NB + n + 1, 1 - par)
                blocks(pe, body)
                down(phase, NB - 1, NJ - 1, False)

            def project(what, use):
                pe.wait_ge(turn_drained, use)
                w, src, rows = {"q": (projT[:, 0, :], xT, P), "k": (projT[:, 1, :], xT, P),
                                "v": (projT[:, 2, :], xT, P), "c1": (cs_w1T[:], xT, DH),
                                "c2": (cs_w2T[:], c1, P)}[what]
                for half in HALVES:
                    ins = nc.tensor.matmul(turn[0:rows, half], w, src[:, half], start=True, stop=True)
                ins.then_inc(turn_filled, 1)

            def spread_v(n, f, par):
                pe.wait_ge(work_drained, WORK_ATTN + n * E + f - 1)
                for half in HALVES:
                    nc.tensor.matmul(work[:, f % 2, half], pick_r[:, f, :], vT_hi[:, par, half],
                                     start=True, stop=False)
                    ins = nc.tensor.matmul(work[:, f % 2, half], pick_r[:, f, :], vT_lo[:, par, half],
                                           start=False, stop=True)
                ins.then_inc(work_filled, 1)

            def out_proj(n, f):
                pe.wait_ge(qS_done, n * E + f + 1)
                if f == 0:
                    pe.wait_ge(yT_done, NB + n)
                for half in HALVES:
                    ins = nc.tensor.matmul(acc[:, half], o_wT[:, f, :], qS[:, f % NP, half],
                                           start=(f == 0), stop=(f == E - 1))
                ins.then_inc(qS_used, 1)

            def attn(n, par, first, last):
                for f in range(E):
                    if f == 0:
                        pe.wait_ge(turn_drained, (turn_first("v") if first else turn_attn(n - 1, "v")) + 1)
                    spread_v(n, f, par)
                    if f == 0:
                        turn_in(turn_attn(n, "in", last), NB + n + 1, 1 - par)
                    if not last:
                        for at, what in ((1, "q"), (2, "k"), (3, "v"), (5, "c1"), (6, "c2")):
                            if f == at:
                                project(what, turn_attn(n, what))
                    if f == 4:
                        turn_out(turn_attn(n, "out", last), NB + n - 1, 1 - par)
                    if f >= LAG:
                        out_proj(n, f - LAG)
                    elif not first:
                        out_proj(n - 1, f - LAG + E)

            turn_in(0, 0, 0)
            ffn(0)
            for what in ("q", "k", "v", "c1", "c2"):
                project(what, turn_first(what))
            blocks(pe, attn)
            for f in range(E - LAG, E):
                out_proj(NB - 1, f)
            ffn(1)
            turn_out(TURN_LAST, 3 * NB - 1, 1)


N_LOADS = 13
SIGNS = 4
PREP_ALL = 4 + 7 + 8 + 1 + 1 + 3
PICKS = 4 + 7 + 8


_INS = ["L0_attn_x", "L0_attn_q_w", "L0_attn_k_w", "L0_attn_v_w", "L0_attn_o_w", "L0_attn_cs_w1", "L0_attn_cs_b1",
        "L0_attn_cs_w2", "L0_attn_cs_b2", "L0_attn_decay_params", "L0_ffn_w1", "L0_ffn_b1", "L0_ffn_w2", "L0_ffn_b2"]


def kernel(**inputs):
    import numpy as _np
    import concourse.bacc as _bacc
    from concourse import mybir as _mybir
    from concourse.bass_utils import run_bass_kernel_spmd as _run

    nc = _bacc.Bacc("TRN2", target_bir_lowering=False, num_devices=1)
    arrays, args = {}, []
    for name in _INS:
        a = _np.ascontiguousarray(inputs[name])
        arrays[f"in_{name}"] = a
        args.append(nc.dram_tensor(f"in_{name}", a.shape, _mybir.dt.from_np(a.dtype), kind="ExternalInput").ap())
    shape = arrays["in_L0_attn_x"].shape
    args.append(nc.dram_tensor("out_0", shape, _mybir.dt.float32, kind="ExternalOutput").ap())
    macaron(nc, *args)
    r = _run(nc, [arrays], core_ids=[0])
    return r.results[0]["out_0"]
```

```python
from contextlib import ExitStack

import concourse.bass as bass
from concourse import mybir

F32 = mybir.dt.float32
F32R = mybir.dt.float32r
ALU = mybir.AluOpType
ACT = mybir.ActivationFunctionType
AX_X = mybir.AxisListType.X

P = 128
BANK = 512
EPS = 1e-5
LAM_MAX = 0.9995


def macaron(nc, x, q_w, k_w, v_w, o_w, cs_w1, cs_b1, cs_w2, cs_b2, decay, w1, b1, w2, b2, out):
    SEQS, T, D = x.shape
    HEADS, E = decay.shape
    DH = cs_w1.shape[0]
    HID = w1.shape[0]
    TOKENS = SEQS * T
    BLK = 2 * BANK
    TILES = BLK // P
    NB = TOKENS // BLK
    NJ = HID // P
    assert D == P and HEADS * E == P and BLK % T == 0 and NB % 2 == 0 and NB >= 4 and NJ % 2 == 0 and E % 4 == 0
    LAG = 3
    DOWN_LAG = 3
    NP = 4

    WORK_FFN = (0, NB * (NJ + E))
    WORK_ATTN = NB * NJ
    TURN_ATTN = 2 * NB + 1
    TURN_FFN2 = TURN_ATTN + 5 + 7 * (NB - 1) + 2

    def turn_ffn(phase, n, what):
        if isinstance(n, int) and n == NB - 1 and what == "out":
            return (TURN_ATTN + 1, TURN_FFN2 + 2 * n)[phase]
        return (1, TURN_FFN2)[phase] + 2 * n + {"in": 0, "out": 1}[what]

    TURN_LAST = TURN_FFN2 + 2 * NB - 1

    def turn_first(what):
        return TURN_ATTN + {"q": -1, "k": 0, "v": 2, "c1": 3, "c2": 4}[what]

    def turn_attn(n, what, last=False):
        order = ["in", "out"] if last else ["in", "q", "k", "v", "out", "c1", "c2"]
        return TURN_ATTN + 5 + 7 * n + order.index(what)

    with ExitStack() as ctx:
        def sb(name, shape, dt=F32):
            return ctx.enter_context(nc.sbuf_tensor(name, shape, dt))

        def sem(name):
            return ctx.enter_context(nc.semaphore(name))

        turn = ctx.enter_context(nc.psum_tensor("turn", [P, BLK], F32))
        work = ctx.enter_context(nc.psum_tensor("work", [P, 2, BLK], F32))
        acc = ctx.enter_context(nc.psum_tensor("acc", [P, BLK], F32))

        x_res = sb("x_res", [P, NB * TILES, D])
        xn = sb("xn", [P, 2, TILES, D])
        bn = sb("bn", [P, 2, TILES, 6])
        neg_mean = sb("neg_mean", [P, 2, TILES])
        neg_mean_rstd = sb("neg_mean_rstd", [P, 2, TILES])
        diff = sb("diff", [P, 2, TILES])
        var_eps = sb("var_eps", [P, 2, TILES])
        rstd = sb("rstd", [P, 2, TILES])
        minus_half = sb("minus_half", [P, TILES])
        warm = sb("warm", [P, TILES])
        xT_hi = sb("xT_hi", [P, 2, BLK], F32R)
        xT_lo = sb("xT_lo", [P, 2, BLK], F32R)
        yT = sb("yT", [P, 2, BLK])
        xT = sb("xT", [P, BLK])
        qT = sb("qT", [P, 2, BLK])
        kT = sb("kT", [P, 2, BLK])
        lam = sb("lam", [P, 2, BLK])
        v_parts = sb("v_parts", [P, 2, 2, BLK], F32R)
        c2 = sb("c2", [P, BLK])
        c1 = c2[0:DH, :]
        state = sb("state", [P, NP, BLK])
        gelu = state
        gelu_hi = sb("gelu_hi", [P, NJ, BLK], F32R)
        gelu_lo = sb("gelu_lo", [P, NJ, BLK], F32R)
        qS = sb("qS", [P, NP, BLK])

        ident = sb("ident", [P, P])
        w1_sb = qS[:, 0, 0:NJ * D].rearrange("p (j d) -> p j d", d=D)
        w2_sb = qS[:, 0, NJ * D:NJ * D + HID]
        neg12 = qS[:, 1, 0:NJ * D + HID]
        sign12 = qS[:, 2, 0:NJ * D + HID]
        abs12 = state[:, 1, 0:NJ * D + HID]
        alpha1 = sb("alpha1", [P, NJ])
        alpha2_half = sb("alpha2_half", [P, 1])
        b1_sb = sb("b1_sb", [P, NJ])
        b1_rows = sb("b1_rows", [NJ, P])
        b2_sb = sb("b2_sb", [P, 1])
        b2_half = sb("b2_half", [P, 1])
        sign1T = sb("sign1T", [P, NJ * P], F32R)
        sign2T = sb("sign2T", [P, NJ * D], F32R)
        proj_sb = state[:, 0, 0:4 * D].rearrange("p (j d) -> p j d", d=D)
        projT = sb("projT", [P, 4, P])
        cs_w1_sb = sb("cs_w1_sb", [DH, D])
        cs_w2_sb = sb("cs_w2_sb", [P, DH])
        v_wT = sb("v_wT", [P, P])
        cs_w1T = sb("cs_w1T", [P, DH])
        cs_w2T = sb("cs_w2T", [DH, P])
        cs_b1_sb = sb("cs_b1_sb", [DH, 1])
        cs_b2_sb = sb("cs_b2_sb", [P, 1])
        cs_b2_half = sb("cs_b2_half", [P, 1])
        decay_sb = sb("decay_sb", [P, 1])
        decay_tanh = sb("decay_tanh", [P, 1])
        lam_scale = sb("lam_scale", [P, 1])
        lam_base = sb("lam_base", [P, 1])
        pick = qS[:, 3, :].rearrange("p (f c) -> p f c", f=E)
        pick_v = sb("pick_v", [P, E // 2, P], F32R)
        o_wT = sb("o_wT", [P, E, D])

        x_load = [sem("x_load_0"), sem("x_load_1")]
        w_ffn_load = sem("w_ffn_load")
        w_attn_load = sem("w_attn_load")
        decay_tanh_done = sem("decay_tanh_done")
        x_store = [sem("x_store_0"), sem("x_store_1")]
        consts = sem("consts")
        prep_dve = sem("prep_dve")
        prep_act = sem("prep_act")
        prep_pe = sem("prep_pe")
        bn_done = sem("bn_done")
        stats_done = sem("stats_done")
        moment_step = sem("moment_step")
        rstd_done = sem("rstd_done")
        shift_done = sem("shift_done")
        xn_done = sem("xn_done")
        turn_filled = sem("turn_filled")
        turn_drained = sem("turn_drained")
        xT_hi_done = sem("xT_hi_done")
        work_filled = sem("work_filled")
        work_drained = sem("work_drained")
        act_hi_done = sem("act_hi_done")
        pool_lo_done = sem("pool_lo_done")
        dve_hi_done = sem("dve_hi_done")
        dve_lo_done = sem("dve_lo_done")
        gelu_used = sem("gelu_used")
        yT_done = sem("yT_done")
        v_hi_done = sem("v_hi_done")
        decay_done = sem("decay_done")
        lam_step = sem("lam_step")
        kv_done = sem("kv_done")
        qS_done = sem("qS_done")
        qS_used = sem("qS_used")

        x_dram = x.rearrange("s t d -> (s t) d").rearrange("(n p) d -> p n d", p=P)
        out_dram = out.rearrange("s t d -> (s t) d").rearrange("(n p) d -> p n d", p=P)
        HALVES = [slice(0, BANK), slice(BANK, BLK)]

        def blocks(eng, body):
            body(0, 0, True, False)
            with eng.Fori(0, (NB - 4) // 2) as i:
                body(i * 2 + 1, 1, False, False)
                body(i * 2 + 2, 0, False, False)
            for n in range(NB - 3, NB):
                body(n, n % 2, False, n == NB - 1)

        block = ctx.enter_context(nc.Block())

        @block.sync
        def _(sp):
            for n in range(NB):
                if n >= 2:
                    sp.wait_ge(x_load[n % 2], 16 * (n // 2))
                sp.dma_start(x_res[:, n * TILES:(n + 1) * TILES, :],
                             x_dram[:, n * TILES:(n + 1) * TILES, :]).then_inc(x_load[n % 2], 16)
            for n in range(NB):
                sp.wait_ge(turn_drained, (turn_ffn(1, n + 1, "out") if n < NB - 1 else TURN_LAST) + 1)
                if n >= 2:
                    sp.wait_ge(x_store[n % 2], 16 * (n // 2))
                sp.dma_start(out_dram[:, n * TILES:(n + 1) * TILES, :],
                             x_res[:, n * TILES:(n + 1) * TILES, :]).then_inc(x_store[n % 2], 16)
            sp.wait_ge(x_store[0], 16 * (NB // 2))
            sp.wait_ge(x_store[1], 16 * (NB // 2))

        @block.gpsimd
        def _(pool):
            nc.gpsimd.memset(minus_half[:], -0.5).then_inc(consts, 1)
            nc.gpsimd.memset(ident[:], 0.0).then_inc(consts, 1)
            pool.wait_ge(consts, 2)
            nc.gpsimd.affine_select(out=ident[:], in_=ident[:], compare_op=ALU.not_equal, fill=1.0, base=0,
                                    pattern=[[-1, P]], channel_multiplier=1).then_inc(consts, 1)
            pool.wait_ge(consts, 3)

            def inverse_std(g, par, for_act=False):
                pool.wait_ge(stats_done, g + 1)
                nc.gpsimd.tensor_tensor(rstd[:, par, :], var_eps[:, par, :], minus_half[:],
                                        ALU.pow).then_inc(rstd_done, 1)
                if for_act:
                    pool.wait_ge(rstd_done, g + 1)
                    nc.gpsimd.tensor_tensor(neg_mean_rstd[:, par, :], neg_mean[:, par, :], rstd[:, par, :],
                                            ALU.mult).then_inc(shift_done, 1)

            inverse_std(0, 0)
            inverse_std(1, 1)

            def ffn(phase):
                def body(n, par, first, last):
                    for j in range(NJ - 1):
                        pool.wait_ge((act_hi_done, dve_hi_done)[j % 2], (phase * NB + n) * (NJ // 2) + j // 2 + 1)
                        nc.gpsimd.tensor_tensor(gelu_lo[:, j, :], gelu[:, j, :], gelu_hi[:, j, :].bitcast(F32),
                                                ALU.subtract).then_inc(pool_lo_done, 1)
                        if j == 1 and not (phase == 1 and isinstance(n, int) and n + 2 >= NB):
                            inverse_std(2 * phase * NB + n + 2, par)
                blocks(pool, body)

            def attn(n, par, first, last):
                for f in range(E):
                    if f == 4:
                        inverse_std(NB + n + 2, par, True)
                    s = n * E + f
                    pool.wait_ge(work_drained, WORK_ATTN + s + 1)
                    if f == 0:
                        pool.wait_ge(turn_drained, (turn_first("q") if first else turn_attn(n - 1, "q")) + 1)
                    if not (first and f < NP):
                        pool.wait_ge(qS_used, s - NP + 1)
                    nc.gpsimd.tensor_tensor(qS[:, f % NP, :], qT[:, par, :], state[:, f % NP, :],
                                            ALU.mult).then_inc(qS_done, 1)

            ffn(0)
            blocks(pool, attn)
            ffn(1)

        @block.scalar
        def _(act):
            loads = [
                (w1_sb, w1.rearrange("(j p) d -> p j d", p=P)), (w2_sb, w2),
                (b1_rows[:], b1.rearrange("(j p) -> j p", p=P)), (b2_sb[:], b2.rearrange("(p a) -> p a", a=1)),
                (proj_sb[:, 0, :], q_w), (proj_sb[:, 1, :], k_w), (proj_sb[:, 2, :], v_w), (proj_sb[:, 3, :], o_w),
                (cs_w1_sb[:], cs_w1), (cs_b1_sb[:], cs_b1.rearrange("(p a) -> p a", a=1)),
                (decay_sb[:], decay.rearrange("h (e a) -> (h e) a", a=1)),
                (cs_w2_sb[:], cs_w2.rearrange("h (a c) -> h a c", a=1).broadcast_to([HEADS, E, DH])),
                (cs_b2_sb[:], cs_b2.rearrange("(h a c) -> h a c", a=1, c=1).broadcast_to([HEADS, E, 1])),
            ]
            for m, (dst, src) in enumerate(loads):
                act.dma_start(dst, src).then_inc(w_ffn_load if m < N_FFN_LOADS else w_attn_load, 16)

            def prep_ffn():
                act.wait_ge(consts, 1)
                nc.scalar.activation(warm[:], minus_half[:], ACT.Gelu).then_inc(prep_act, 1)
                act.wait_ge(w_ffn_load, 16 * N_FFN_LOADS)
                for j in range(NJ):
                    nc.scalar.activation(abs12[:, j * D:(j + 1) * D], w1_sb[:, j, :], ACT.Abs,
                                         accum_out=alpha1[:, j:j + 1]).then_inc(prep_act, 1)
                nc.scalar.activation(abs12[:, NJ * D:NJ * D + HID], w2_sb, ACT.Abs,
                                     accum_out=alpha2_half[:, 0:1]).then_inc(prep_act, 1)
                act.wait_ge(prep_act, NJ + 2)
                nc.scalar.mul(alpha1[:], alpha1[:], 1.0 / D).then_inc(prep_act, 1)
                nc.scalar.mul(alpha2_half[:], alpha2_half[:], 0.5 / HID).then_inc(prep_act, 1)
                act.wait_ge(prep_pe, 1)
                nc.scalar.copy(sign1T[:], work[:, 0, 0:NJ * P]).then_inc(prep_act, 1)
                nc.scalar.copy(sign2T[:], work[:, 0, NJ * P:NJ * P + NJ * D]).then_inc(prep_act, 1)
                nc.scalar.copy(b1_sb[:], work[:, 1, 0:NJ]).then_inc(prep_act, 1)

            def prep_attn():
                act.wait_ge(w_attn_load, 16 * (N_LOADS - N_FFN_LOADS))
                nc.scalar.activation(decay_tanh[:], decay_sb[:], ACT.Tanh, scale=0.5).then_inc(decay_tanh_done, 1)
                nc.scalar.mul(cs_b2_half[:], cs_b2_sb[:], 0.5).then_inc(prep_act, 1)
                act.wait_ge(prep_pe, 2)
                nc.scalar.copy(projT[:].rearrange("p a b -> p (a b)"), acc[:, 0:4 * P]).then_inc(prep_act, 1)
                nc.scalar.copy(v_wT[:].rearrange("p (f h) -> p f h", h=HEADS),
                               acc[:, 2 * P:3 * P].rearrange("p (h f) -> p f h", f=E)).then_inc(prep_act, 1)
                nc.scalar.copy(cs_w1T[:], acc[:, BANK:BANK + DH]).then_inc(prep_act, 1)
                nc.scalar.copy(cs_w2T[:], acc[0:DH, BANK + P:BANK + 2 * P]).then_inc(prep_act, 1)

            def prep_out():
                act.wait_ge(prep_pe, 3)
                nc.scalar.copy(o_wT[:].rearrange("p a b -> p (a b)"), acc[:]).then_inc(prep_act, 1)
                act.wait_ge(prep_dve, PREP_DVE)

            def split_hi(use, par):
                act.wait_ge(turn_filled, use + 1)
                nc.scalar.copy(xT_hi[:, par, :], turn[:]).then_inc(xT_hi_done, 1)

            def keep_xT(use):
                act.wait_ge(turn_filled, use + 1)
                nc.scalar.copy(xT[:], turn[:]).then_inc(turn_drained, 1)

            def result(par, read, count, scale, bias):
                act.wait_ge(read, count)
                if scale is None:
                    nc.scalar.copy(yT[:, par, :], acc[:]).then_inc(yT_done, 1)
                else:
                    nc.scalar.activation(yT[:, par, :], acc[:], ACT.Identity, bias=bias,
                                         scale=scale).then_inc(yT_done, 1)

            def ffn(phase):
                def body(n, par, first, last):
                    for j in range(NJ):
                        s = WORK_FFN[phase] + n * NJ + j
                        act.wait_ge(work_filled, s + 1)
                        if not (phase == 0 and first):
                            act.wait_ge(gelu_used, (phase * NB + n - 1) * NJ + j + 1)
                        nc.scalar.activation(gelu[:, j, :], work[:, j % 2, :], ACT.Gelu,
                                             bias=b1_sb[:, j:j + 1], scale=alpha1[:, j:j + 1]
                                             ).then_inc(work_drained, 1)
                        if phase == 0 and first and j == 0:
                            prep_out()
                        if j == 2 and not first:
                            result(1 - par, gelu_used, (phase * NB + n) * NJ, alpha2_half[:, 0:1], b2_half[:, 0:1])
                        if j % 2 == 0:
                            act.wait_ge(work_drained, s + 1)
                            nc.scalar.copy(gelu_hi[:, j, :], gelu[:, j, :]).then_inc(act_hi_done, 1)
                        if j == 1 and not (phase == 1 and last):
                            use = turn_ffn(phase, n, "in")
                            if last:
                                keep_xT(use)
                            else:
                                split_hi(use, 1 - par)
                        if phase == 0 and last and j >= 2:
                            project(("q", "k")[j - 2], turn_first(("q", "k")[j - 2]), 0, None)
                blocks(act, body)
                if phase == 0:
                    project("v", turn_first("v"), 0, None)
                    project("c1", turn_first("c1"), 0, None)
                result(1, gelu_used, (phase + 1) * NB * NJ, alpha2_half[:, 0:1], b2_half[:, 0:1])
                if phase == 0:
                    project("c2", turn_first("c2"), 0, None)

            def project(what, use, par, n):
                act.wait_ge(turn_filled, use + 1)
                if what == "q":
                    if n is not None and not (isinstance(n, int) and n == 0):
                        act.wait_ge(qS_done, n * E)
                    nc.scalar.copy(qT[:, par, :], turn[:]).then_inc(turn_drained, 1)
                elif what == "k":
                    if n is not None and not (isinstance(n, int) and n == 0):
                        act.wait_ge(kv_done, n * E)
                    nc.scalar.copy(kT[:, par, :], turn[:]).then_inc(turn_drained, 1)
                elif what == "v":
                    for a in (0, 1):
                        ins = nc.scalar.copy(v_parts[0:P // 2, par, a, :], turn[a * P // 2:(a + 1) * P // 2, :])
                    ins.then_inc(v_hi_done, 1)
                elif what == "c1":
                    if n is not None:
                        act.wait_ge(lam_step, 2 * n + 2)
                    nc.scalar.activation(c1, turn[0:DH, :], ACT.Tanh, bias=cs_b1_sb[:, 0:1]
                                         ).then_inc(turn_drained, 1)
                elif what == "c2":
                    nc.scalar.activation(c2[:], turn[:], ACT.Tanh, bias=cs_b2_half[:, 0:1], scale=0.5
                                         ).then_inc(turn_drained, 1)
                    act.wait_ge(turn_drained, use + 1)
                    nc.scalar.activation(c2[:], c2[:], ACT.Identity, bias=lam_base[:, 0:1],
                                         scale=lam_scale[:, 0:1]).then_inc(decay_done, 1)

            def normalise(g, n, par):
                for t in range(TILES):
                    m = n * TILES + t
                    src = x_res[:, m:m + 1, :] if isinstance(m, int) else x_res[:, bass.ds(m, 1), :]
                    ins = nc.scalar.activation(xn[:, par, t, :], src, ACT.Identity,
                                               bias=neg_mean_rstd[:, par, t:t + 1], scale=rstd[:, par, t:t + 1])
                ins.then_inc(xn_done, 1)

            def attn(n, par, first, last):
                for f in range(E):
                    if f == 0:
                        use = turn_attn(n, "in", last)
                        if last:
                            split_hi(use, 1 - par)
                        else:
                            keep_xT(use)
                    if f == 3 and not first:
                        result(1 - par, qS_used, n * E, None, None)
                    if f == 4:
                        act.wait_ge(shift_done, n + 1)
                        act.wait_ge(consts, 3)
                        normalise(NB + n + 2, n + 2 - (NB if isinstance(n, int) and n + 2 >= NB else 0), par)
                    if not last:
                        for at, what in ((1, "q"), (2, "k"), (3, "v"), (5, "c1"), (6, "c2")):
                            if f == at:
                                project(what, turn_attn(n, what), 1 - par, n)

            prep_ffn()
            split_hi(0, 0)
            prep_attn()
            ffn(0)
            blocks(act, attn)
            result(1, qS_used, NB * E, None, None)
            ffn(1)

        @block.vector
        def _(dve):
            step = [0]

            def prep(ins, wait=True):
                ins.then_inc(prep_dve, 1)
                step[0] += 1
                if wait:
                    dve.wait_ge(prep_dve, step[0])

            def prep_signs():
                dve.wait_ge(w_ffn_load, 16 * N_FFN_LOADS)
                w12 = qS[:, 0, :]
                prep(nc.vector.tensor_scalar(neg12, w12, 0.0, None, ALU.is_lt))
                prep(nc.vector.scalar_tensor_tensor(sign12, w12, 0.0, neg12, ALU.is_gt, ALU.subtract))

            def prep_picks():
                dve.wait_ge(consts, 3)
                for f in range(E):
                    src = ident[:].rearrange("p (h e) -> p h e", e=E)[:, :, f:f + 1].broadcast_to([P, HEADS, E])
                    prep(nc.vector.tensor_copy(pick[:, f, :].rearrange("p (h e) -> p h e", e=E), src), False)
                for g in range(E // 2):
                    hi, lo = (ident[:, o + g * HEADS:o + (g + 1) * HEADS].rearrange("p (h a) -> p h a", a=1)
                              .broadcast_to([P, HEADS, E]) for o in (0, P // 2))
                    prep(nc.vector.tensor_tensor(pick_v[:, g, :].rearrange("p (h e) -> p h e", e=E), hi, lo,
                                                 ALU.add), False)

            def prep_rest():
                prep(nc.vector.tensor_scalar(b2_half[:], b2_sb[:], 0.5, None, ALU.mult), False)
                dve.wait_ge(decay_tanh_done, 1)
                prep(nc.vector.tensor_scalar(decay_tanh[:], decay_tanh[:], 0.5, 0.5, ALU.mult, ALU.add))
                prep(nc.vector.tensor_scalar(lam_scale[:], decay_tanh[:], 0.1, None, ALU.mult), False)
                prep(nc.vector.tensor_scalar(lam_base[:], decay_tanh[:], 1.1, None, ALU.mult), False)
                assert step[0] == PREP_DVE

            def tile_stats(g, n, par, first, count):
                for t in range(first, first + count):
                    ins = nc.vector.bn_stats(bn[:, par, t, :], x_res[:, tile(n, t), :])
                if first + count == TILES:
                    ins.then_inc(bn_done, 1)

            def moments_sum(g, n, par):
                mean_e, mean_o, m2_e, m2_o = (bn[:, par, :, k] for k in (1, 4, 2, 5))
                dve.wait_ge(bn_done, g + 1)
                nc.vector.tensor_tensor(neg_mean[:, par, :], mean_e, mean_o, ALU.add)
                nc.vector.tensor_tensor(diff[:, par, :], mean_e, mean_o, ALU.subtract)
                nc.vector.scalar_tensor_tensor(var_eps[:, par, :], m2_e, EPS * D, m2_o, ALU.add, ALU.add
                                               ).then_inc(moment_step, 1)

            def moments_mean(g, n, par):
                dve.wait_ge(moment_step, 2 * g + 1)
                nc.vector.tensor_scalar(neg_mean[:, par, :], neg_mean[:, par, :], -0.5, None, ALU.mult)
                nc.vector.scalar_tensor_tensor(diff[:, par, :], diff[:, par, :], 0.25, diff[:, par, :],
                                               ALU.mult, ALU.mult).then_inc(moment_step, 1)

            def moments_var(g, n, par):
                dve.wait_ge(moment_step, 2 * g + 2)
                nc.vector.scalar_tensor_tensor(var_eps[:, par, :], var_eps[:, par, :], 1.0 / D, diff[:, par, :],
                                               ALU.mult, ALU.add).then_inc(stats_done, 1)

            def statistics(g, n, par):
                tile_stats(g, n, par, 0, TILES)
                for part in (moments_sum, moments_mean, moments_var):
                    part(g, n, par)

            def normalise(g, n, par):
                dve.wait_ge(rstd_done, g + 1)
                for t in range(TILES):
                    ins = nc.vector.tensor_scalar(xn[:, par, t, :], x_res[:, tile(n, t), :],
                                                  neg_mean[:, par, t:t + 1], rstd[:, par, t:t + 1],
                                                  ALU.add, ALU.mult)
                ins.then_inc(xn_done, 1)

            def tile(n, t):
                return bass.ds(n * TILES + t, 1) if not isinstance(n, int) else slice(n * TILES + t, n * TILES + t + 1)

            def tiles(n):
                return bass.ds(n * TILES, TILES) if not isinstance(n, int) else slice(n * TILES, (n + 1) * TILES)

            def add_result(use, n):
                dve.wait_ge(turn_filled, use + 1)
                nc.vector.tensor_tensor(x_res[:, tiles(n), :], x_res[:, tiles(n), :],
                                        turn[:].rearrange("p (t d) -> p t d", d=D), ALU.add
                                        ).then_inc(turn_drained, 1)

            def split_lo(par, count, hi, lo, hi_done, uses=1):
                dve.wait_ge(hi_done, count)
                nc.vector.tensor_tensor(lo[:, par, :], turn[:], hi[:, par, :].bitcast(F32), ALU.subtract
                                        ).then_inc(turn_drained, uses)

            def split_v_lo(par, count):
                dve.wait_ge(v_hi_done, count)
                for a in (0, 1):
                    ins = nc.vector.tensor_tensor(v_parts[P // 2:P, par, a, :], turn[a * P // 2:(a + 1) * P // 2, :],
                                                  v_parts[0:P // 2, par, a, :].bitcast(F32), ALU.subtract)
                ins.then_inc(turn_drained, 1)

            def gelu_hi_part(phase, n, j):
                dve.wait_ge(work_drained, WORK_FFN[phase] + n * NJ + j + 1)
                nc.vector.tensor_copy(gelu_hi[:, j, :], gelu[:, j, :]).then_inc(dve_hi_done, 1)

            def gelu_lo_part(phase, n):
                j = NJ - 1
                dve.wait_ge(dve_hi_done, (phase * NB + n) * (NJ // 2) + j // 2 + 1)
                nc.vector.tensor_tensor(gelu_lo[:, j, :], gelu[:, j, :], gelu_hi[:, j, :].bitcast(F32), ALU.subtract
                                        ).then_inc(dve_lo_done, 1)

            def next_norm(phase, n, par, part):
                ahead = n + 2
                if isinstance(n, int) and ahead >= NB:
                    ahead -= NB
                    if phase == 2:
                        return
                part(phase * NB + n + 2, ahead, par)

            def ffn(phase):
                def body(n, par, first, last):
                    gelu_hi_part(phase, n, 1)
                    next_norm(2 * phase, n, par, lambda g, m, p: tile_stats(g, m, p, 0, TILES // 2))
                    if not last:
                        split_lo(1 - par, phase * NB + n + 2, xT_hi, xT_lo, xT_hi_done,
                                 2 if phase == 0 and first else 1)
                    next_norm(2 * phase, n, par, lambda g, m, p: tile_stats(g, m, p, TILES // 2, TILES // 2))
                    for part in (moments_sum, moments_mean, moments_var):
                        next_norm(2 * phase, n, par, part)
                    if not (phase == 0 and first):
                        add_result(turn_ffn(phase, n, "out"), NB - 1 if first else n - 1)
                    next_norm(2 * phase, n, par, normalise)
                    gelu_hi_part(phase, n, NJ - 1)
                    gelu_lo_part(phase, n)
                return body

            prep_picks()
            dve.wait_ge(x_load[0], 16)
            statistics(0, 0, 0)
            prep_signs()
            normalise(0, 0, 0)
            dve.wait_ge(x_load[1], 16)
            statistics(1, 1, 1)
            split_lo(0, 1, xT_hi, xT_lo, xT_hi_done)
            normalise(1, 1, 1)
            prep_rest()

            def ffn_first():
                dve.wait_ge(x_load[0], 16 * 2)
                ffn(0)(0, 0, True, False)
                with dve.Fori(0, (NB - 4) // 2) as i:
                    for half in (0, 1):
                        dve.wait_ge(x_load[1 - half], 16 * (i + 2 + half))
                        ffn(0)(i * 2 + 1 + half, 1 - half, False, False)
                for n in range(NB - 3, NB):
                    if n + 2 < NB:
                        dve.wait_ge(x_load[n % 2], 16 * ((n + 2) // 2 + 1))
                    ffn(0)(n, n % 2, False, n == NB - 1)

            def decay_of(par, count, m):
                dve.wait_ge(decay_done, m + 1)
                nc.vector.tensor_scalar(lam[:, par, :], c2[:], LAM_MAX, 0.0, ALU.min, ALU.max
                                        ).then_inc(lam_step, 1)
                dve.wait_ge(lam_step, count + 1)
                nc.vector.memset(lam[:, par, :].rearrange("p (s t) -> p s t", t=T)[:, :, 0:1], 0.0
                                 ).then_inc(lam_step, 1)

            def attn(n, par, first, last):
                for f in range(E):
                    s = WORK_ATTN + n * E + f
                    dve.wait_ge(work_filled, s + 1)
                    nc.vector.tensor_tensor(work[:, f % 2, :], work[:, f % 2, :], kT[:, par, :], ALU.mult
                                            ).then_inc(kv_done, 1)
                    if f < 2:
                        next_norm(1, n, par, lambda g, m, p: tile_stats(g, m, p, f * TILES // 2, TILES // 2))
                    elif f == 2:
                        next_norm(1, n, par, moments_sum)
                        next_norm(1, n, par, moments_mean)
                    elif f == 3:
                        next_norm(1, n, par, moments_var)
                    if f == 0 and not first:
                        decay_of(par, n * 2, n)
                    if not (first and f < NP):
                        dve.wait_ge(qS_done, n * E + f - NP + 1)
                    if f == 0:
                        dve.wait_ge(lam_step, n * 2 + 2)
                    dve.wait_ge(kv_done, n * E + f + 1)
                    nc.vector.tensor_tensor_scan(state[:, f % NP, :], lam[:, par, :], work[:, f % 2, :], 0.0,
                                                 ALU.mult, ALU.add).then_inc(work_drained, 1)
                    if f == 0 and last:
                        split_lo(1 - par, NB + 1, xT_hi, xT_lo, xT_hi_done)
                    if f == 3 and not last:
                        split_v_lo(1 - par, n + 2)
                    if f == 4:
                        add_result(turn_attn(n, "out", last), NB - 1 if first else n - 1)
            ffn_first()
            split_v_lo(0, 1)
            decay_of(0, 0, 0)
            blocks(dve, attn)
            blocks(dve, ffn(1))
            add_result(TURN_LAST, NB - 1)

        @block.tensor
        def _(pe):
            def turn_tiles(dst, src_of, ins_of=None):
                for t in range(TILES):
                    ins = nc.tensor.transpose(dst[:, t * P:(t + 1) * P], src_of(t), ident[:])
                return ins

            def prep_ffn():
                pe.wait_ge(consts, 3)
                pe.wait_ge(prep_dve, SIGNS)
                for j in range(NJ + HID // P):
                    nc.tensor.transpose(work[:, 0, j * P:(j + 1) * P], sign12[:, j * P:(j + 1) * P], ident[:])
                nc.tensor.transpose(work[:, 1, 0:NJ], b1_rows[:], ident[0:NJ, 0:NJ]).then_inc(prep_pe, 1)

            def prep_attn():
                pe.wait_ge(w_attn_load, 16 * (N_LOADS - N_FFN_LOADS))
                for j in range(4):
                    nc.tensor.transpose(acc[:, j * P:(j + 1) * P], proj_sb[:, j, :], ident[:])
                nc.tensor.transpose(acc[:, BANK:BANK + DH], cs_w1_sb[:], ident[0:DH, 0:DH])
                nc.tensor.transpose(acc[0:DH, BANK + P:BANK + 2 * P], cs_w2_sb[:], ident[:]).then_inc(prep_pe, 1)

            def prep_out():
                pe.wait_ge(prep_act, PREP_ACT - 1)
                pe.wait_ge(prep_dve, PICKS)
                for f in range(E):
                    ins = nc.tensor.matmul(acc[:, f * P:(f + 1) * P], pick[:, f, :], projT[:, 3, :],
                                           start=True, stop=True)
                ins.then_inc(prep_pe, 1)

            def turn_in(use, g, par, uses=1):
                pe.wait_ge(xn_done, g + 1)
                if not (isinstance(use, int) and use == 0):
                    pe.wait_ge(turn_drained, use)
                turn_tiles(turn, lambda t: xn[:, par, t, :]).then_inc(turn_filled, uses)

            def turn_out(use, g, par):
                pe.wait_ge(yT_done, g + 1)
                pe.wait_ge(turn_drained, use)
                turn_tiles(turn, lambda t: yT[:, par, t * P:(t + 1) * P]).then_inc(turn_filled, 1)

            def hidden(phase, n, j, par, first):
                s = WORK_FFN[phase] + n * NJ + j
                if not (phase == 0 and first and j < 2):
                    pe.wait_ge(work_drained, s - 1)
                for half in HALVES:
                    w = sign1T[:, j * P:(j + 1) * P]
                    nc.tensor.matmul(work[:, j % 2, half], w, xT_hi[:, par, half], start=True, stop=False)
                    ins = nc.tensor.matmul(work[:, j % 2, half], w, xT_lo[:, par, half], start=False, stop=True)
                ins.then_inc(work_filled, 1)

            def down(phase, n, j, first):
                if j < NJ - 1:
                    pe.wait_ge(pool_lo_done, (phase * NB + n) * (NJ - 1) + j + 1)
                else:
                    pe.wait_ge(dve_lo_done, phase * NB + n + 1)
                if j == 0 and not (phase == 0 and first):
                    pe.wait_ge(yT_done, 2 * phase * NB + n)
                for half in HALVES:
                    w = sign2T[:, j * D:(j + 1) * D]
                    nc.tensor.matmul(acc[:, half], w, gelu_hi[:, j, half], start=(j == 0), stop=False)
                    ins = nc.tensor.matmul(acc[:, half], w, gelu_lo[:, j, half], start=False, stop=(j == NJ - 1))
                ins.then_inc(gelu_used, 1)

            def ffn(phase):
                def body(n, par, first, last):
                    for j in range(NJ):
                        if j == 0:
                            use = (turn_ffn(phase, n - 1, "in") if not first
                                   else 0 if phase == 0 else turn_attn(NB - 1, "in", True))
                            pe.wait_ge(turn_drained, use + 1)
                        hidden(phase, n, j, par, first)
                        if phase == 0 and first and j == 0:
                            prep_out()
                        if phase == 0 and first and j == DOWN_LAG:
                            pe.wait_ge(prep_act, PREP_ACT)
                        if j == 1 and not (phase == 1 and last):
                            turn_in(turn_ffn(phase, n, "in"), 2 * phase * NB + n + 1, 1 - par,
                                    2 if phase == 0 and first else 1)
                        if phase == 0 and last and j >= 2:
                            project(("q", "k")[j - 2], turn_first(("q", "k")[j - 2]))
                        if j >= DOWN_LAG:
                            down(phase, n, j - DOWN_LAG, first)
                        elif not first:
                            down(phase, n - 1, j - DOWN_LAG + NJ, False)
                        if j == NJ - 1 and not (phase == 0 and first):
                            turn_out(turn_ffn(phase, n, "out"), 2 * phase * NB + n - 1, 1 - par)
                blocks(pe, body)
                for m, j in enumerate(range(NJ - DOWN_LAG, NJ)):
                    down(phase, NB - 1, j, False)
                    if phase == 0:
                        project(("v", "c1", "c2")[m], turn_first(("v", "c1", "c2")[m]))

            def project(what, use):
                pe.wait_ge(turn_drained, use)
                w, src, rows = {"q": (projT[:, 0, :], xT, P), "k": (projT[:, 1, :], xT, P),
                                "v": (v_wT[:], xT, P), "c1": (cs_w1T[:], xT, DH),
                                "c2": (cs_w2T[:], c1, P)}[what]
                for half in HALVES:
                    ins = nc.tensor.matmul(turn[0:rows, half], w, src[:, half], start=True, stop=True)
                ins.then_inc(turn_filled, 1)

            def spread_v(n, f, par):
                pe.wait_ge(work_drained, WORK_ATTN + n * E + f - 1)
                for half in HALVES:
                    ins = nc.tensor.matmul(work[:, f % 2, half], pick_v[:, f % (E // 2), :],
                                           v_parts[:, par, f // (E // 2), half], start=True, stop=True)
                ins.then_inc(work_filled, 1)

            def out_proj(n, f):
                pe.wait_ge(qS_done, n * E + f + 1)
                if f == 0:
                    pe.wait_ge(yT_done, NB + n)
                for half in HALVES:
                    ins = nc.tensor.matmul(acc[:, half], o_wT[:, f, :], qS[:, f % NP, half],
                                           start=(f == 0), stop=(f == E - 1))
                ins.then_inc(qS_used, 1)

            def attn(n, par, first, last):
                for f in range(E):
                    if f == 0:
                        pe.wait_ge(turn_drained, (turn_first("v") if first else turn_attn(n - 1, "v")) + 1)
                    spread_v(n, f, par)
                    if f == 0:
                        turn_in(turn_attn(n, "in", last), NB + n + 1, 1 - par)
                    if not last and 1 <= f <= 3:
                        what = ("q", "k", "v")[f - 1]
                        project(what, turn_attn(n, what))
                    if f >= LAG:
                        out_proj(n, f - LAG)
                    elif not first:
                        out_proj(n - 1, f - LAG + E)
                    if f == 4:
                        turn_out(turn_attn(n, "out", last), NB + n - 1, 1 - par)
                    if not last and 5 <= f <= 6:
                        what = ("c1", "c2")[f - 5]
                        project(what, turn_attn(n, what))

            prep_ffn()
            turn_in(0, 0, 0)
            prep_attn()
            pe.wait_ge(prep_act, PREP_FFN)
            ffn(0)
            blocks(pe, attn)
            for f in range(E - LAG, E):
                out_proj(NB - 1, f)
            ffn(1)
            turn_out(TURN_LAST, 3 * NB - 1, 1)


N_LOADS, N_FFN_LOADS = 13, 4
PICKS = 8
SIGNS = PICKS + 4 + 2
PREP_DVE = SIGNS + 4
PREP_FFN = 1 + 4 + 1 + 2 + 3
PREP_ACT = PREP_FFN + 1 + 5


_INS = ["L0_attn_x", "L0_attn_q_w", "L0_attn_k_w", "L0_attn_v_w", "L0_attn_o_w", "L0_attn_cs_w1", "L0_attn_cs_b1",
        "L0_attn_cs_w2", "L0_attn_cs_b2", "L0_attn_decay_params", "L0_ffn_w1", "L0_ffn_b1", "L0_ffn_w2", "L0_ffn_b2"]


def kernel(**inputs):
    import numpy as _np
    import concourse.bacc as _bacc
    from concourse import mybir as _mybir
    from concourse.bass_utils import run_bass_kernel_spmd as _run

    nc = _bacc.Bacc("TRN2", target_bir_lowering=False, num_devices=1)
    arrays, args = {}, []
    for name in _INS:
        a = _np.ascontiguousarray(inputs[name])
        arrays[f"in_{name}"] = a
        args.append(nc.dram_tensor(f"in_{name}", a.shape, _mybir.dt.from_np(a.dtype), kind="ExternalInput").ap())
    shape = arrays["in_L0_attn_x"].shape
    args.append(nc.dram_tensor("out_0", shape, _mybir.dt.float32, kind="ExternalOutput").ap())
    macaron(nc, *args)
    r = _run(nc, [arrays], core_ids=[0])
    return r.results[0]["out_0"]
```

```python
from contextlib import ExitStack

import concourse.bass as bass
from concourse import mybir

F32 = mybir.dt.float32
F32R = mybir.dt.float32r
ALU = mybir.AluOpType
ACT = mybir.ActivationFunctionType
AX_X = mybir.AxisListType.X

P = 128
BANK = 512
EPS = 1e-5
LAM_MAX = 0.9995


def macaron(nc, x, q_w, k_w, v_w, o_w, cs_w1, cs_b1, cs_w2, cs_b2, decay, w1, b1, w2, b2, out):
    SEQS, T, D = x.shape
    HEADS, E = decay.shape
    DH = cs_w1.shape[0]
    HID = w1.shape[0]
    TOKENS = SEQS * T
    BLK = 2 * BANK
    TILES = BLK // P
    NB = TOKENS // BLK
    NJ = HID // P
    assert D == P and HEADS * E == P and BLK % T == 0 and NB % 2 == 0 and NB >= 4 and NJ % 2 == 0 and E % 4 == 0
    REP = P // DH
    assert REP == 4
    LAG = 3
    DOWN_LAG = 3
    ACT_TILES = 2
    NP = 4

    WORK_FFN = (0, NB * (NJ + E))
    WORK_ATTN = NB * NJ
    TURN_ATTN = 2 * NB + 1
    TURN_FFN2 = TURN_ATTN + 5 + 7 * (NB - 1) + 2

    def turn_ffn(phase, n, what):
        if isinstance(n, int) and n == NB - 1 and what == "out":
            return (TURN_ATTN + 1, TURN_FFN2 + 2 * n)[phase]
        return (1, TURN_FFN2)[phase] + 2 * n + {"in": 0, "out": 1}[what]

    TURN_LAST = TURN_FFN2 + 2 * NB - 1

    def turn_first(what):
        return TURN_ATTN + {"q": -1, "k": 0, "c1": 2, "v": 3, "c2": 4}[what]

    def turn_attn(n, what, last=False):
        order = ["in", "out"] if last else ["in", "q", "k", "c1", "v", "out", "c2"]
        return TURN_ATTN + 5 + 7 * n + order.index(what)

    with ExitStack() as ctx:
        def sb(name, shape, dt=F32):
            return ctx.enter_context(nc.sbuf_tensor(name, shape, dt))

        def sem(name):
            return ctx.enter_context(nc.semaphore(name))

        turn = ctx.enter_context(nc.psum_tensor("turn", [P, BLK], F32))
        work = ctx.enter_context(nc.psum_tensor("work", [P, 2, BLK], F32))
        acc = ctx.enter_context(nc.psum_tensor("acc", [P, BLK], F32))

        x_res = sb("x_res", [P, NB * TILES, D])
        xn = sb("xn", [P, 2, TILES, D])
        bn = sb("bn", [P, 2, TILES, 6])
        neg_mean = sb("neg_mean", [P, 2, TILES])
        neg_mean_rstd = sb("neg_mean_rstd", [P, 2, TILES])
        diff = sb("diff", [P, 2, TILES])
        var_eps = sb("var_eps", [P, 2, TILES])
        rstd = sb("rstd", [P, 2, TILES])
        minus_half = sb("minus_half", [P, TILES])
        warm = sb("warm", [P, TILES])
        xT_hi = sb("xT_hi", [P, 2, BLK], F32R)
        xT_lo = sb("xT_lo", [P, 2, BLK], F32R)
        yT = sb("yT", [P, 2, BLK])
        xT = sb("xT", [P, BLK])
        qT = sb("qT", [P, 2, BLK])
        kT = sb("kT", [P, 2, BLK])
        lam = sb("lam", [P, 2, BLK])
        v_parts = sb("v_parts", [P, 2, 2, BLK], F32R)
        c2 = sb("c2", [P, BLK])
        c1 = c2
        c1_parts = xT_lo[:, 0, :]
        state = sb("state", [P, NP, BLK])
        gelu = state
        gelu_hi = sb("gelu_hi", [P, NJ, BLK], F32R)
        gelu_lo = sb("gelu_lo", [P, NJ, BLK], F32R)
        qS = sb("qS", [P, NP, BLK])

        ident = sb("ident", [P, P])
        w1_sb = qS[:, 0, 0:NJ * D].rearrange("p (j d) -> p j d", d=D)
        w2_sb = qS[:, 0, NJ * D:NJ * D + HID]
        neg12 = qS[:, 1, 0:NJ * D + HID]
        sign12 = qS[:, 2, 0:NJ * D + HID]
        abs12 = state[:, 1, 0:NJ * D + HID]
        alpha1 = sb("alpha1", [P, NJ])
        alpha2_half = sb("alpha2_half", [P, 1])
        b1_sb = sb("b1_sb", [P, NJ])
        b1_rows = sb("b1_rows", [NJ, P])
        b2_sb = sb("b2_sb", [P, 1])
        b2_half = sb("b2_half", [P, 1])
        sign1T = sb("sign1T", [P, NJ * P], F32R)
        sign2T = sb("sign2T", [P, NJ * D], F32R)
        proj_sb = state[:, 0, 0:4 * D].rearrange("p (j d) -> p j d", d=D)
        projT = sb("projT", [P, 4, P])
        cs_w1_sb = sb("cs_w1_sb", [P, D])
        cs_w2_sb = sb("cs_w2_sb", [P, DH])
        v_wT = sb("v_wT", [P, P])
        cs_w2_parts = sb("cs_w2_parts", [P, REP, DH], F32R)
        cs_w1T = sb("cs_w1T", [P, P])
        cs_w2T = sb("cs_w2T", [P, P], F32R)
        cs_b1_sb = sb("cs_b1_sb", [P, 1])
        cs_b2_sb = sb("cs_b2_sb", [P, 1])
        cs_b2_half = sb("cs_b2_half", [P, 1])
        decay_sb = sb("decay_sb", [P, 1])
        decay_tanh = sb("decay_tanh", [P, 1])
        lam_scale = sb("lam_scale", [P, 1])
        lam_base = sb("lam_base", [P, 1])
        pick = qS[:, 3, :].rearrange("p (f c) -> p f c", f=E)
        pick_v = sb("pick_v", [P, E // 2, P], F32R)
        o_wT = sb("o_wT", [P, E, D])

        x_load = [sem("x_load_0"), sem("x_load_1")]
        w_ffn_load = sem("w_ffn_load")
        w_attn_load = sem("w_attn_load")
        decay_tanh_done = sem("decay_tanh_done")
        x_store = [sem("x_store_0"), sem("x_store_1")]
        consts = sem("consts")
        prep_dve = sem("prep_dve")
        prep_act = sem("prep_act")
        prep_pe = sem("prep_pe")
        bn_done = sem("bn_done")
        stats_done = sem("stats_done")
        moment_step = sem("moment_step")
        rstd_done = sem("rstd_done")
        shift_done = sem("shift_done")
        xn_dve_done = sem("xn_dve_done")
        xn_act_done = sem("xn_act_done")
        turn_filled = sem("turn_filled")
        turn_drained = sem("turn_drained")
        xT_hi_done = sem("xT_hi_done")
        work_filled = sem("work_filled")
        work_drained = sem("work_drained")
        act_hi_done = sem("act_hi_done")
        pool_lo_done = sem("pool_lo_done")
        dve_hi_done = sem("dve_hi_done")
        dve_lo_done = sem("dve_lo_done")
        gelu_used = sem("gelu_used")
        first_half_done = sem("first_half_done")
        yT_done = sem("yT_done")
        v_hi_done = sem("v_hi_done")
        w2_hi_done = sem("w2_hi_done")
        w2_lo_done = sem("w2_lo_done")
        c1_hi_done = sem("c1_hi_done")
        c1_lo_done = sem("c1_lo_done")
        decay_done = sem("decay_done")
        lam_step = sem("lam_step")
        kv_done = sem("kv_done")
        qS_done = sem("qS_done")
        qS_used = sem("qS_used")

        x_dram = x.rearrange("s t d -> (s t) d").rearrange("(n p) d -> p n d", p=P)
        out_dram = out.rearrange("s t d -> (s t) d").rearrange("(n p) d -> p n d", p=P)
        HALVES = [slice(0, BANK), slice(BANK, BLK)]

        def blocks(eng, body):
            body(0, 0, True, False)
            with eng.Fori(0, (NB - 4) // 2) as i:
                body(i * 2 + 1, 1, False, False)
                body(i * 2 + 2, 0, False, False)
            for n in range(NB - 3, NB):
                body(n, n % 2, False, n == NB - 1)

        def blocks_landed(eng, body):
            eng.wait_ge(x_load[0], 16 * 2)
            body(0, 0, True, False)
            with eng.Fori(0, (NB - 4) // 2) as i:
                for half in (0, 1):
                    eng.wait_ge(x_load[1 - half], 16 * (i + 2 + half))
                    body(i * 2 + 1 + half, 1 - half, False, False)
            for n in range(NB - 3, NB):
                if n + 2 < NB:
                    eng.wait_ge(x_load[n % 2], 16 * ((n + 2) // 2 + 1))
                body(n, n % 2, False, n == NB - 1)

        block = ctx.enter_context(nc.Block())

        @block.sync
        def _(sp):
            for n in range(NB):
                if n >= 2:
                    sp.wait_ge(x_load[n % 2], 16 * (n // 2))
                sp.dma_start(x_res[:, n * TILES:(n + 1) * TILES, :],
                             x_dram[:, n * TILES:(n + 1) * TILES, :]).then_inc(x_load[n % 2], 16)
            for n in range(NB):
                sp.wait_ge(turn_drained, (turn_ffn(1, n + 1, "out") if n < NB - 1 else TURN_LAST) + 1)
                if n >= 2:
                    sp.wait_ge(x_store[n % 2], 16 * (n // 2))
                sp.dma_start(out_dram[:, n * TILES:(n + 1) * TILES, :],
                             x_res[:, n * TILES:(n + 1) * TILES, :]).then_inc(x_store[n % 2], 16)
            sp.wait_ge(x_store[0], 16 * (NB // 2))
            sp.wait_ge(x_store[1], 16 * (NB // 2))

        @block.gpsimd
        def _(pool):
            nc.gpsimd.memset(minus_half[:], -0.5).then_inc(consts, 1)
            nc.gpsimd.memset(ident[:], 0.0).then_inc(consts, 1)
            pool.wait_ge(consts, 2)
            nc.gpsimd.affine_select(out=ident[:], in_=ident[:], compare_op=ALU.not_equal, fill=1.0, base=0,
                                    pattern=[[-1, P]], channel_multiplier=1).then_inc(consts, 1)
            pool.wait_ge(consts, 3)

            def inverse_std(g, par):
                if not (isinstance(g, int) and g < 3):
                    pool.wait_ge(xn_act_done, g - 2)
                pool.wait_ge(stats_done, g + 1)
                nc.gpsimd.tensor_tensor(rstd[:, par, :], var_eps[:, par, :], minus_half[:],
                                        ALU.pow).then_inc(rstd_done, 1)
                pool.wait_ge(rstd_done, g + 1)
                nc.gpsimd.tensor_tensor(neg_mean_rstd[:, par, :], neg_mean[:, par, :], rstd[:, par, :],
                                        ALU.mult).then_inc(shift_done, 1)

            def split_c1_lo(m, before, count):
                pool.wait_ge(before, count)
                pool.wait_ge(c1_hi_done, m + 1)
                nc.gpsimd.tensor_tensor(c1_parts[P // 2:P, :], c1[P // 2:P, :], c1_parts[P // 2:P, :].bitcast(F32),
                                        ALU.subtract).then_inc(c1_lo_done, 1)
                pool.wait_ge(c1_lo_done, m + 1)

            inverse_std(0, 0)
            pool.wait_ge(w2_hi_done, REP // 2)
            for a in range(1, REP, 2):
                nc.gpsimd.tensor_tensor(cs_w2_parts[:, a, :], cs_w2_sb[:], cs_w2_parts[:, a - 1, :].bitcast(F32),
                                        ALU.subtract).then_inc(w2_lo_done, 1)
            inverse_std(1, 1)

            def ffn(phase):
                def body(n, par, first, last):
                    for j in range(NJ - 1):
                        pool.wait_ge((act_hi_done, dve_hi_done)[j % 2], (phase * NB + n) * (NJ // 2) + j // 2 + 1)
                        nc.gpsimd.tensor_tensor(gelu_lo[:, j, :], gelu[:, j, :], gelu_hi[:, j, :].bitcast(F32),
                                                ALU.subtract).then_inc(pool_lo_done, 1)
                        if j == 1 and not (phase == 1 and isinstance(n, int) and n + 2 >= NB):
                            inverse_std(2 * phase * NB + n + 2, par)
                blocks(pool, body)

            def attn(n, par, first, last):
                for f in range(E):
                    if f == 4:
                        inverse_std(NB + n + 2, par)
                    if f == 5 and not last:
                        split_c1_lo(n + 1, qS_done, n * E + f)
                    s = n * E + f
                    pool.wait_ge(work_drained, WORK_ATTN + s + 1)
                    if f == 0:
                        pool.wait_ge(turn_drained, (turn_first("q") if first else turn_attn(n - 1, "q")) + 1)
                    if not (first and f < NP):
                        pool.wait_ge(qS_used, s - NP + 1)
                    nc.gpsimd.tensor_tensor(qS[:, f % NP, :], qT[:, par, :], state[:, f % NP, :],
                                            ALU.mult).then_inc(qS_done, 1)

            ffn(0)
            split_c1_lo(0, pool_lo_done, NB * (NJ - 1))
            blocks(pool, attn)
            ffn(1)

        @block.scalar
        def _(act):
            loads = [
                (w1_sb, w1.rearrange("(j p) d -> p j d", p=P)), (w2_sb, w2),
                (b1_rows[:], b1.rearrange("(j p) -> j p", p=P)), (b2_sb[:], b2.rearrange("(p a) -> p a", a=1)),
                (proj_sb[:, 0, :], q_w), (proj_sb[:, 1, :], k_w), (proj_sb[:, 2, :], v_w), (proj_sb[:, 3, :], o_w),
                (cs_w1_sb[:], cs_w1.rearrange("(r j) d -> r j d", r=1).broadcast_to([REP, DH, D])),
                (cs_b1_sb[:], cs_b1.rearrange("(r j a) -> r j a", r=1, a=1).broadcast_to([REP, DH, 1])),
                (decay_sb[:], decay.rearrange("h (e a) -> (h e) a", a=1)),
                (cs_w2_sb[:], cs_w2.rearrange("h (a c) -> h a c", a=1).broadcast_to([HEADS, E, DH])),
                (cs_b2_sb[:], cs_b2.rearrange("(h a c) -> h a c", a=1, c=1).broadcast_to([HEADS, E, 1])),
            ]
            for m, (dst, src) in enumerate(loads):
                act.dma_start(dst, src).then_inc(w_ffn_load if m < N_FFN_LOADS else w_attn_load, 16)

            def prep_ffn():
                act.wait_ge(consts, 1)
                nc.scalar.activation(warm[:], minus_half[:], ACT.Gelu).then_inc(prep_act, 1)
                act.wait_ge(w_ffn_load, 16 * N_FFN_LOADS)
                for j in range(NJ):
                    nc.scalar.activation(abs12[:, j * D:(j + 1) * D], w1_sb[:, j, :], ACT.Abs,
                                         accum_out=alpha1[:, j:j + 1]).then_inc(prep_act, 1)
                nc.scalar.activation(abs12[:, NJ * D:NJ * D + HID], w2_sb, ACT.Abs,
                                     accum_out=alpha2_half[:, 0:1]).then_inc(prep_act, 1)
                act.wait_ge(prep_act, NJ + 2)
                nc.scalar.mul(alpha1[:], alpha1[:], 1.0 / D).then_inc(prep_act, 1)
                nc.scalar.mul(alpha2_half[:], alpha2_half[:], 0.5 / HID).then_inc(prep_act, 1)
                act.wait_ge(w_attn_load, 16 * (N_LOADS - N_FFN_LOADS))
                for a in range(0, REP, 2):
                    nc.scalar.copy(cs_w2_parts[:, a, :], cs_w2_sb[:]).then_inc(w2_hi_done, 1)
                act.wait_ge(prep_pe, 1)
                nc.scalar.copy(sign1T[:], work[:, 0, 0:NJ * P]).then_inc(prep_act, 1)
                nc.scalar.copy(sign2T[:], work[:, 0, NJ * P:NJ * P + NJ * D]).then_inc(prep_act, 1)
                nc.scalar.copy(b1_sb[:], work[:, 1, 0:NJ]).then_inc(prep_act, 1)

            def prep_attn():
                act.wait_ge(w_attn_load, 16 * (N_LOADS - N_FFN_LOADS))
                nc.scalar.activation(decay_tanh[:], decay_sb[:], ACT.Tanh, scale=0.5).then_inc(decay_tanh_done, 1)
                nc.scalar.mul(cs_b2_half[:], cs_b2_sb[:], 0.5).then_inc(prep_act, 1)
                act.wait_ge(prep_pe, 2)
                nc.scalar.copy(projT[:].rearrange("p a b -> p (a b)"), acc[:, 0:4 * P]).then_inc(prep_act, 1)
                nc.scalar.copy(v_wT[:].rearrange("p (f h) -> p f h", h=HEADS),
                               acc[:, 2 * P:3 * P].rearrange("p (h f) -> p f h", f=E)).then_inc(prep_act, 1)
                nc.scalar.copy(cs_w1T[:], acc[:, BANK:BANK + P]).then_inc(prep_act, 1)
                nc.scalar.copy(cs_w2T[:], acc[:, BANK + P:BANK + 2 * P]).then_inc(prep_act, 1)

            def prep_out():
                act.wait_ge(prep_pe, 3)
                nc.scalar.copy(o_wT[:].rearrange("p a b -> p (a b)"), acc[:]).then_inc(prep_act, 1)
                act.wait_ge(prep_dve, PREP_DVE)

            def split_hi(use, par):
                act.wait_ge(turn_filled, use + 1)
                nc.scalar.copy(xT_hi[:, par, :], turn[:]).then_inc(xT_hi_done, 1)

            def keep_xT(use):
                act.wait_ge(turn_filled, use + 1)
                nc.scalar.copy(xT[:], turn[:]).then_inc(turn_drained, 1)

            def result_attn(par, count):
                act.wait_ge(qS_used, count)
                nc.scalar.copy(yT[:, par, :], acc[:]).then_inc(yT_done, 2)

            def result_ffn(par, b):
                act.wait_ge(first_half_done, b + 1)
                nc.scalar.activation(yT[:, par, HALVES[0]], acc[:, HALVES[0]], ACT.Identity, bias=b2_half[:, 0:1],
                                     scale=alpha2_half[:, 0:1]).then_inc(yT_done, 1)
                act.wait_ge(gelu_used, (b + 1) * NJ)
                nc.scalar.activation(yT[:, par, HALVES[1]], acc[:, HALVES[1]], ACT.Identity, bias=b2_half[:, 0:1],
                                     scale=alpha2_half[:, 0:1]).then_inc(yT_done, 1)

            def normalise(phase, n, par, count):
                ahead = n + 2
                if isinstance(n, int) and ahead >= NB:
                    ahead -= NB
                    if phase == 2:
                        return
                act.wait_ge(shift_done, phase * NB + n + 3)
                act.wait_ge(consts, 3)
                for t in range(TILES - count, TILES):
                    m = ahead * TILES + t
                    src = x_res[:, m:m + 1, :] if isinstance(m, int) else x_res[:, bass.ds(m, 1), :]
                    ins = nc.scalar.activation(xn[:, par, t, :], src, ACT.Identity,
                                               bias=neg_mean_rstd[:, par, t:t + 1], scale=rstd[:, par, t:t + 1])
                ins.then_inc(xn_act_done, 1)

            def ffn(phase):
                def body(n, par, first, last):
                    for j in range(NJ):
                        s = WORK_FFN[phase] + n * NJ + j
                        act.wait_ge(work_filled, s + 1)
                        if not (phase == 0 and first):
                            act.wait_ge(gelu_used, (phase * NB + n - 1) * NJ + j + 1)
                        nc.scalar.activation(gelu[:, j, :], work[:, j % 2, :], ACT.Gelu,
                                             bias=b1_sb[:, j:j + 1], scale=alpha1[:, j:j + 1]
                                             ).then_inc(work_drained, 1)
                        if phase == 0 and first and j == 0:
                            prep_out()
                        if j == 2 and not first:
                            result_ffn(1 - par, phase * NB + n - 1)
                        if j % 2 == 0:
                            act.wait_ge(work_drained, s + 1)
                            nc.scalar.copy(gelu_hi[:, j, :], gelu[:, j, :]).then_inc(act_hi_done, 1)
                        if j == 1 and not (phase == 1 and last):
                            use = turn_ffn(phase, n, "in")
                            if last:
                                keep_xT(use)
                            else:
                                split_hi(use, 1 - par)
                        if phase == 0 and last and j >= 2:
                            project(("q", "k")[j - 2], turn_first(("q", "k")[j - 2]), 0, None)
                        if j == NJ - 1:
                            normalise(2 * phase, n, par, ACT_TILES)
                if phase == 0:
                    blocks_landed(act, body)
                else:
                    blocks(act, body)
                if phase == 0:
                    project("c1", turn_first("c1"), 0, None)
                    project("v", turn_first("v"), 0, None)
                result_ffn(1, (phase + 1) * NB - 1)
                if phase == 0:
                    project("c2", turn_first("c2"), 0, None)

            def project(what, use, par, n):
                act.wait_ge(turn_filled, use + 1)
                if what == "q":
                    if n is not None and not (isinstance(n, int) and n == 0):
                        act.wait_ge(qS_done, n * E)
                    nc.scalar.copy(qT[:, par, :], turn[:]).then_inc(turn_drained, 1)
                elif what == "k":
                    if n is not None and not (isinstance(n, int) and n == 0):
                        act.wait_ge(kv_done, n * E)
                    nc.scalar.copy(kT[:, par, :], turn[:]).then_inc(turn_drained, 1)
                elif what == "v":
                    for a in (0, 1):
                        nc.scalar.copy(v_parts[0:P // 2, par, a, :], turn[a * P // 2:(a + 1) * P // 2, :]
                                       ).then_inc(v_hi_done, 1)
                elif what == "c1":
                    if n is not None:
                        act.wait_ge(lam_step, 2 * n + 2)
                    nc.scalar.activation(c1[:], turn[:], ACT.Tanh, bias=cs_b1_sb[:, 0:1]
                                         ).then_inc(turn_drained, 1)
                    act.wait_ge(turn_drained, use + 1)
                    nc.scalar.copy(c1_parts, c1[:]).then_inc(c1_hi_done, 1)
                elif what == "c2":
                    nc.scalar.activation(c2[:], turn[:], ACT.Tanh, bias=cs_b2_half[:, 0:1], scale=0.5
                                         ).then_inc(turn_drained, 1)
                    act.wait_ge(turn_drained, use + 1)
                    nc.scalar.activation(c2[:], c2[:], ACT.Identity, bias=lam_base[:, 0:1],
                                         scale=lam_scale[:, 0:1]).then_inc(decay_done, 1)

            def attn(n, par, first, last):
                for f in range(E):
                    if f == 0:
                        use = turn_attn(n, "in", last)
                        if last:
                            split_hi(use, 1 - par)
                        else:
                            keep_xT(use)
                    if f == 3 and not first:
                        result_attn(1 - par, n * E)
                    if f == 5:
                        normalise(1, n, par, TILES)
                    if not last:
                        for at, what in ((1, "q"), (2, "k"), (3, "c1"), (4, "v"), (6, "c2")):
                            if f == at:
                                project(what, turn_attn(n, what), 1 - par, n)

            prep_ffn()
            split_hi(0, 0)
            prep_attn()
            ffn(0)
            blocks(act, attn)
            result_attn(1, NB * E)
            ffn(1)

        @block.vector
        def _(dve):
            step = [0]

            def prep(ins, wait=True):
                ins.then_inc(prep_dve, 1)
                step[0] += 1
                if wait:
                    dve.wait_ge(prep_dve, step[0])

            def prep_signs():
                dve.wait_ge(w_ffn_load, 16 * N_FFN_LOADS)
                w12 = qS[:, 0, :]
                prep(nc.vector.tensor_scalar(neg12, w12, 0.0, None, ALU.is_lt))
                prep(nc.vector.scalar_tensor_tensor(sign12, w12, 0.0, neg12, ALU.is_gt, ALU.subtract))

            def prep_picks():
                dve.wait_ge(consts, 3)
                for f in range(E):
                    src = ident[:].rearrange("p (h e) -> p h e", e=E)[:, :, f:f + 1].broadcast_to([P, HEADS, E])
                    prep(nc.vector.tensor_copy(pick[:, f, :].rearrange("p (h e) -> p h e", e=E), src), False)
                for g in range(E // 2):
                    hi, lo = (ident[:, o + g * HEADS:o + (g + 1) * HEADS].rearrange("p (h a) -> p h a", a=1)
                              .broadcast_to([P, HEADS, E]) for o in (0, P // 2))
                    prep(nc.vector.tensor_tensor(pick_v[:, g, :].rearrange("p (h e) -> p h e", e=E), hi, lo,
                                                 ALU.add), False)

            def prep_rest():
                prep(nc.vector.tensor_scalar(b2_half[:], b2_sb[:], 0.5, None, ALU.mult), False)
                dve.wait_ge(decay_tanh_done, 1)
                prep(nc.vector.tensor_scalar(decay_tanh[:], decay_tanh[:], 0.5, 0.5, ALU.mult, ALU.add))
                prep(nc.vector.tensor_scalar(lam_scale[:], decay_tanh[:], 0.1, None, ALU.mult), False)
                prep(nc.vector.tensor_scalar(lam_base[:], decay_tanh[:], 1.1, None, ALU.mult), False)
                assert step[0] == PREP_DVE

            def tile_stats(g, n, par, first, count):
                for t in range(first, first + count):
                    ins = nc.vector.bn_stats(bn[:, par, t, :], x_res[:, tile(n, t), :])
                if first + count == TILES:
                    ins.then_inc(bn_done, 1)

            def moments_sum(g, n, par):
                mean_e, mean_o, m2_e, m2_o = (bn[:, par, :, k] for k in (1, 4, 2, 5))
                dve.wait_ge(bn_done, g + 1)
                nc.vector.tensor_tensor(neg_mean[:, par, :], mean_e, mean_o, ALU.add)
                nc.vector.tensor_tensor(diff[:, par, :], mean_e, mean_o, ALU.subtract)
                nc.vector.scalar_tensor_tensor(var_eps[:, par, :], m2_e, EPS * D, m2_o, ALU.add, ALU.add
                                               ).then_inc(moment_step, 1)

            def moments_mean(g, n, par):
                dve.wait_ge(moment_step, 2 * g + 1)
                nc.vector.tensor_scalar(neg_mean[:, par, :], neg_mean[:, par, :], -0.5, None, ALU.mult)
                nc.vector.scalar_tensor_tensor(diff[:, par, :], diff[:, par, :], 0.25, diff[:, par, :],
                                               ALU.mult, ALU.mult).then_inc(moment_step, 1)

            def moments_var(g, n, par):
                dve.wait_ge(moment_step, 2 * g + 2)
                nc.vector.scalar_tensor_tensor(var_eps[:, par, :], var_eps[:, par, :], 1.0 / D, diff[:, par, :],
                                               ALU.mult, ALU.add).then_inc(stats_done, 1)

            def statistics(g, n, par):
                tile_stats(g, n, par, 0, TILES)
                for part in (moments_sum, moments_mean, moments_var):
                    part(g, n, par)

            def normalise(g, n, par, count=TILES - ACT_TILES):
                dve.wait_ge(rstd_done, g + 1)
                for t in range(count):
                    ins = nc.vector.tensor_scalar(xn[:, par, t, :], x_res[:, tile(n, t), :],
                                                  neg_mean[:, par, t:t + 1], rstd[:, par, t:t + 1],
                                                  ALU.add, ALU.mult)
                ins.then_inc(xn_dve_done, 1)

            def tile(n, t):
                return bass.ds(n * TILES + t, 1) if not isinstance(n, int) else slice(n * TILES + t, n * TILES + t + 1)

            def tiles(n):
                return bass.ds(n * TILES, TILES) if not isinstance(n, int) else slice(n * TILES, (n + 1) * TILES)

            def add_result(use, n):
                dve.wait_ge(turn_filled, use + 1)
                nc.vector.tensor_tensor(x_res[:, tiles(n), :], x_res[:, tiles(n), :],
                                        turn[:].rearrange("p (t d) -> p t d", d=D), ALU.add
                                        ).then_inc(turn_drained, 1)

            def split_lo(par, count, hi, lo, hi_done, uses=1):
                dve.wait_ge(hi_done, count)
                nc.vector.tensor_tensor(lo[:, par, :], turn[:], hi[:, par, :].bitcast(F32), ALU.subtract
                                        ).then_inc(turn_drained, uses)

            def split_v_lo(par, count):
                for a in (0, 1):
                    dve.wait_ge(v_hi_done, 2 * count - 1 + a)
                    ins = nc.vector.tensor_tensor(v_parts[P // 2:P, par, a, :], turn[a * P // 2:(a + 1) * P // 2, :],
                                                  v_parts[0:P // 2, par, a, :].bitcast(F32), ALU.subtract)
                ins.then_inc(turn_drained, 1)

            def gelu_hi_part(phase, n, j):
                dve.wait_ge(work_drained, WORK_FFN[phase] + n * NJ + j + 1)
                nc.vector.tensor_copy(gelu_hi[:, j, :], gelu[:, j, :]).then_inc(dve_hi_done, 1)

            def gelu_lo_part(phase, n):
                j = NJ - 1
                dve.wait_ge(dve_hi_done, (phase * NB + n) * (NJ // 2) + j // 2 + 1)
                nc.vector.tensor_tensor(gelu_lo[:, j, :], gelu[:, j, :], gelu_hi[:, j, :].bitcast(F32), ALU.subtract
                                        ).then_inc(dve_lo_done, 1)

            def next_norm(phase, n, par, part):
                ahead = n + 2
                if isinstance(n, int) and ahead >= NB:
                    ahead -= NB
                    if phase == 2:
                        return
                part(phase * NB + n + 2, ahead, par)

            def ffn(phase):
                def body(n, par, first, last):
                    gelu_hi_part(phase, n, 1)
                    next_norm(2 * phase, n, par, statistics)
                    if not last:
                        split_lo(1 - par, phase * NB + n + 2, xT_hi, xT_lo, xT_hi_done,
                                 2 if phase == 0 and first else 1)
                    next_norm(2 * phase, n, par, normalise)
                    if not (phase == 0 and first):
                        add_result(turn_ffn(phase, n, "out"), NB - 1 if first else n - 1)
                    gelu_hi_part(phase, n, NJ - 1)
                    gelu_lo_part(phase, n)
                return body

            prep_picks()
            dve.wait_ge(x_load[0], 16)
            statistics(0, 0, 0)
            prep_signs()
            normalise(0, 0, 0, TILES)
            dve.wait_ge(x_load[1], 16)
            statistics(1, 1, 1)
            split_lo(0, 1, xT_hi, xT_lo, xT_hi_done)
            normalise(1, 1, 1, TILES)
            prep_rest()

            def decay_of(par, count, m):
                dve.wait_ge(decay_done, m + 1)
                nc.vector.tensor_scalar(lam[:, par, :], c2[:], LAM_MAX, 0.0, ALU.min, ALU.max
                                        ).then_inc(lam_step, 1)
                dve.wait_ge(lam_step, count + 1)
                nc.vector.memset(lam[:, par, :].rearrange("p (s t) -> p s t", t=T)[:, :, 0:1], 0.0
                                 ).then_inc(lam_step, 1)

            def attn(n, par, first, last):
                for f in range(E):
                    s = WORK_ATTN + n * E + f
                    dve.wait_ge(work_filled, s + 1)
                    nc.vector.tensor_tensor(work[:, f % 2, :], work[:, f % 2, :], kT[:, par, :], ALU.mult
                                            ).then_inc(kv_done, 1)
                    if f < 2:
                        next_norm(1, n, par, lambda g, m, p: tile_stats(g, m, p, f * TILES // 2, TILES // 2))
                    elif f == 2:
                        next_norm(1, n, par, moments_sum)
                        next_norm(1, n, par, moments_mean)
                    elif f == 3:
                        next_norm(1, n, par, moments_var)
                    if f == 0 and not first:
                        decay_of(par, n * 2, n)
                    if not (first and f < NP):
                        dve.wait_ge(qS_done, n * E + f - NP + 1)
                    if f == 0:
                        dve.wait_ge(lam_step, n * 2 + 2)
                    dve.wait_ge(kv_done, n * E + f + 1)
                    nc.vector.tensor_tensor_scan(state[:, f % NP, :], lam[:, par, :], work[:, f % 2, :], 0.0,
                                                 ALU.mult, ALU.add).then_inc(work_drained, 1)
                    if f == 0 and last:
                        split_lo(1 - par, NB + 1, xT_hi, xT_lo, xT_hi_done)
                    if f == 4 and not last:
                        split_v_lo(1 - par, n + 2)
                    if f == 5:
                        add_result(turn_attn(n, "out", last), NB - 1 if first else n - 1)
            blocks_landed(dve, ffn(0))
            split_v_lo(0, 1)
            decay_of(0, 0, 0)
            blocks(dve, attn)
            blocks(dve, ffn(1))
            add_result(TURN_LAST, NB - 1)

        @block.tensor
        def _(pe):
            def turn_tiles(dst, src_of):
                for t in range(TILES):
                    ins = nc.tensor.transpose(dst[:, t * P:(t + 1) * P], src_of(t), ident[:])
                return ins

            def prep_ffn():
                pe.wait_ge(consts, 3)
                pe.wait_ge(prep_dve, SIGNS)
                for j in range(NJ + HID // P):
                    nc.tensor.transpose(work[:, 0, j * P:(j + 1) * P], sign12[:, j * P:(j + 1) * P], ident[:])
                nc.tensor.transpose(work[:, 1, 0:NJ], b1_rows[:], ident[0:NJ, 0:NJ]).then_inc(prep_pe, 1)

            def prep_attn():
                pe.wait_ge(w_attn_load, 16 * (N_LOADS - N_FFN_LOADS))
                for j in range(4):
                    nc.tensor.transpose(acc[:, j * P:(j + 1) * P], proj_sb[:, j, :], ident[:])
                nc.tensor.transpose(acc[:, BANK:BANK + P], cs_w1_sb[:], ident[:])
                pe.wait_ge(w2_lo_done, REP // 2)
                nc.tensor.transpose(acc[:, BANK + P:BANK + 2 * P],
                                    cs_w2_parts[:].rearrange("p r j -> p (r j)").bitcast(F32),
                                    ident[:]).then_inc(prep_pe, 1)

            def prep_out():
                pe.wait_ge(prep_act, PREP_ACT - 1)
                pe.wait_ge(prep_dve, PICKS)
                for f in range(E):
                    ins = nc.tensor.matmul(acc[:, f * P:(f + 1) * P], pick[:, f, :], projT[:, 3, :],
                                           start=True, stop=True)
                ins.then_inc(prep_pe, 1)

            def turn_in(use, g, par, uses=1, shared=True, shared_from=0):
                if isinstance(g, int) and g < 2:
                    pe.wait_ge(xn_dve_done, g + 1)
                else:
                    pe.wait_ge(xn_act_done, g - 1)
                    if shared:
                        pe.wait_ge(xn_dve_done, g + 1 - shared_from)
                if not (isinstance(use, int) and use == 0):
                    pe.wait_ge(turn_drained, use)
                turn_tiles(turn, lambda t: xn[:, par, t, :]).then_inc(turn_filled, uses)

            def turn_out(use, g, par):
                pe.wait_ge(yT_done, 2 * (g + 1))
                pe.wait_ge(turn_drained, use)
                turn_tiles(turn, lambda t: yT[:, par, t * P:(t + 1) * P]).then_inc(turn_filled, 1)

            def hidden(phase, n, j, par, first):
                s = WORK_FFN[phase] + n * NJ + j
                if not (phase == 0 and first and j < 2):
                    pe.wait_ge(work_drained, s - 1)
                for half in HALVES:
                    w = sign1T[:, j * P:(j + 1) * P]
                    nc.tensor.matmul(work[:, j % 2, half], w, xT_hi[:, par, half], start=True, stop=False)
                    ins = nc.tensor.matmul(work[:, j % 2, half], w, xT_lo[:, par, half], start=False, stop=True)
                ins.then_inc(work_filled, 1)

            def down(phase, n, j, first):
                if j < NJ - 1:
                    pe.wait_ge(pool_lo_done, (phase * NB + n) * (NJ - 1) + j + 1)
                else:
                    pe.wait_ge(dve_lo_done, phase * NB + n + 1)
                for h, half in enumerate(HALVES):
                    if j == 0 and not (phase == 0 and first):
                        pe.wait_ge(yT_done, 4 * phase * NB + 2 * n - 1 + h)
                    w = sign2T[:, j * D:(j + 1) * D]
                    nc.tensor.matmul(acc[:, half], w, gelu_hi[:, j, half], start=(j == 0), stop=False)
                    ins = nc.tensor.matmul(acc[:, half], w, gelu_lo[:, j, half], start=False, stop=(j == NJ - 1))
                    if j == NJ - 1 and h == 0:
                        ins.then_inc(first_half_done, 1)
                ins.then_inc(gelu_used, 1)

            def ffn(phase):
                def body(n, par, first, last):
                    for j in range(NJ):
                        if j == 0:
                            use = (turn_ffn(phase, n - 1, "in") if not first
                                   else 0 if phase == 0 else turn_attn(NB - 1, "in", True))
                            pe.wait_ge(turn_drained, use + 1)
                        hidden(phase, n, j, par, first)
                        if phase == 0 and first and j == 0:
                            prep_out()
                        if phase == 0 and first and j == DOWN_LAG:
                            pe.wait_ge(prep_act, PREP_ACT)
                        if j == 1 and not (phase == 1 and last):
                            turn_in(turn_ffn(phase, n, "in"), 2 * phase * NB + n + 1, 1 - par,
                                    2 if phase == 0 and first else 1,
                                    shared=not (phase == 1 and first), shared_from=phase * NB)
                        if phase == 0 and last and j >= 2:
                            project(("q", "k")[j - 2], turn_first(("q", "k")[j - 2]))
                        if j >= DOWN_LAG:
                            down(phase, n, j - DOWN_LAG, first)
                        elif not first:
                            down(phase, n - 1, j - DOWN_LAG + NJ, False)
                        if j == NJ - 1 and not (phase == 0 and first):
                            turn_out(turn_ffn(phase, n, "out"), 2 * phase * NB + n - 1, 1 - par)
                blocks(pe, body)
                for m, j in enumerate(range(NJ - DOWN_LAG, NJ)):
                    down(phase, NB - 1, j, False)
                    if phase == 0:
                        project(("c1", "v", "c2")[m], turn_first(("c1", "v", "c2")[m]))

            def project(what, use, m=0):
                pe.wait_ge(turn_drained, use)
                if what == "c2":
                    pe.wait_ge(c1_lo_done, m + 1)
                w, src = {"q": (projT[:, 0, :], xT), "k": (projT[:, 1, :], xT), "v": (v_wT[:], xT),
                          "c1": (cs_w1T[:], xT), "c2": (cs_w2T[:], c1_parts)}[what]
                for half in HALVES:
                    ins = nc.tensor.matmul(turn[:, half], w, src[:, half], start=True, stop=True)
                ins.then_inc(turn_filled, 1)

            def spread_v(n, f, par):
                pe.wait_ge(work_drained, WORK_ATTN + n * E + f - 1)
                for half in HALVES:
                    ins = nc.tensor.matmul(work[:, f % 2, half], pick_v[:, f % (E // 2), :],
                                           v_parts[:, par, f // (E // 2), half], start=True, stop=True)
                ins.then_inc(work_filled, 1)

            def out_proj(n, f):
                pe.wait_ge(qS_done, n * E + f + 1)
                if f == 0:
                    pe.wait_ge(yT_done, 2 * (NB + n))
                for half in HALVES:
                    ins = nc.tensor.matmul(acc[:, half], o_wT[:, f, :], qS[:, f % NP, half],
                                           start=(f == 0), stop=(f == E - 1))
                ins.then_inc(qS_used, 1)

            def attn(n, par, first, last):
                for f in range(E):
                    if f == 0:
                        pe.wait_ge(turn_drained, (turn_first("v") if first else turn_attn(n - 1, "v")) + 1)
                    spread_v(n, f, par)
                    if f == 0:
                        turn_in(turn_attn(n, "in", last), NB + n + 1, 1 - par, shared=first)
                    if not last and 1 <= f <= 4:
                        what = ("q", "k", "c1", "v")[f - 1]
                        project(what, turn_attn(n, what))
                    if f >= LAG:
                        out_proj(n, f - LAG)
                    elif not first:
                        out_proj(n - 1, f - LAG + E)
                    if f == 5:
                        turn_out(turn_attn(n, "out", last), NB + n - 1, 1 - par)
                    if not last and f == 6:
                        project("c2", turn_attn(n, "c2"), n + 1)

            prep_ffn()
            turn_in(0, 0, 0)
            prep_attn()
            pe.wait_ge(prep_act, PREP_FFN)
            ffn(0)
            blocks(pe, attn)
            for f in range(E - LAG, E):
                out_proj(NB - 1, f)
            ffn(1)
            turn_out(TURN_LAST, 3 * NB - 1, 1)


N_LOADS, N_FFN_LOADS = 13, 4
PICKS = 8
SIGNS = PICKS + 4 + 2
PREP_DVE = SIGNS + 4
PREP_FFN = 1 + 4 + 1 + 2 + 3
PREP_ACT = PREP_FFN + 1 + 5


_INS = ["L0_attn_x", "L0_attn_q_w", "L0_attn_k_w", "L0_attn_v_w", "L0_attn_o_w", "L0_attn_cs_w1", "L0_attn_cs_b1",
        "L0_attn_cs_w2", "L0_attn_cs_b2", "L0_attn_decay_params", "L0_ffn_w1", "L0_ffn_b1", "L0_ffn_w2", "L0_ffn_b2"]


def kernel(**inputs):
    import numpy as _np
    import concourse.bacc as _bacc
    from concourse import mybir as _mybir
    from concourse.bass_utils import run_bass_kernel_spmd as _run

    nc = _bacc.Bacc("TRN2", target_bir_lowering=False, num_devices=1)
    arrays, args = {}, []
    for name in _INS:
        a = _np.ascontiguousarray(inputs[name])
        arrays[f"in_{name}"] = a
        args.append(nc.dram_tensor(f"in_{name}", a.shape, _mybir.dt.from_np(a.dtype), kind="ExternalInput").ap())
    shape = arrays["in_L0_attn_x"].shape
    args.append(nc.dram_tensor("out_0", shape, _mybir.dt.float32, kind="ExternalOutput").ap())
    macaron(nc, *args)
    r = _run(nc, [arrays], core_ids=[0])
    return r.results[0]["out_0"]
```
